# Optimizing a Trainium2 kernel written in Bass

```python
import numpy as np
import jax
import jax.numpy as jnp

def _softmax(x, axis=-1):
    return jax.nn.softmax(x, axis=axis)

def _gelu(x):
    return jax.nn.gelu(x, approximate=True)

def _silu(x):
    return jax.nn.silu(x)

def _sigmoid(x):
    return jax.nn.sigmoid(x)

def _layernorm(x, axis=-1, eps=1e-05):
    m = jnp.mean(x, axis=axis, keepdims=True)
    v = jnp.var(x, axis=axis, keepdims=True)
    return (x - m) / jnp.sqrt(v + eps)

def _scatter_add(tgt, idx, src, axis=0):
    return tgt.at[idx].add(src)

def _segment_sum(src, seg, n):
    return jax.ops.segment_sum(src, seg, n)
kernel_name = 'mk_prb_d1_jaxref_r8_12fb4c'

def setup_inputs(seed: int=0):
    np.random.seed(seed)
    _w = jnp.asarray

    def _L0_attn_setup():
        import jax, jax.numpy as jnp
        import numpy as np
        D_MODEL = 128
        N_HEAD = 16
        D_HEAD = D_MODEL // N_HEAD
        N_CTX = 256
        ROPE_BASE = 10000.0
        SCALE = 1

        def _rope_cache(seq_len, d_head, dtype=jnp.float32):
            inv_freq = 1.0 / ROPE_BASE ** (jnp.arange(0, d_head, 2, dtype=jnp.float32) / d_head)
            t = jnp.arange(seq_len, dtype=jnp.float32)
            freqs = jnp.outer(t, inv_freq)
            emb = jnp.concatenate([freqs, freqs], -1)
            cos = jnp.cos(emb)[None, :, None, :].astype(dtype)
            sin = jnp.sin(emb)[None, :, None, :].astype(dtype)
            return (cos, sin)

        def _apply_rope(x, cos, sin):
            x_even = x[..., 0::2]
            x_odd = x[..., 1::2]
            x_rot = jnp.stack([-x_odd, x_even], axis=-1).reshape(x.shape)
            return x * cos + x_rot * sin

        def _rmsnorm(x, w):
            eps = jnp.finfo(x.dtype).eps
            var = jnp.mean(jnp.square(x), axis=-1, keepdims=True)
            return x * jax.lax.rsqrt(var + eps) * w
        key = jax.random.key(seed)
        ks = jax.random.split(key, 9)
        B, S = (2, N_CTX)
        x = jax.random.normal(ks[0], (B, S, D_MODEL), jnp.float32)
        s = 0.02
        Wq = jax.random.normal(ks[1], (D_MODEL, D_MODEL), jnp.float32) * s
        bq = jax.random.normal(ks[2], (D_MODEL,), jnp.float32) * s
        Wk = jax.random.normal(ks[3], (D_MODEL, D_MODEL), jnp.float32) * s
        bk = jax.random.normal(ks[4], (D_MODEL,), jnp.float32) * s
        Wv = jax.random.normal(ks[5], (D_MODEL, D_MODEL), jnp.float32) * s
        bv = jax.random.normal(ks[6], (D_MODEL,), jnp.float32) * s
        Wo = jax.random.normal(ks[7], (D_MODEL, D_MODEL), jnp.float32) * s
        norm_w = jnp.ones((D_HEAD,), jnp.float32)
        return {'x': x, 'Wq': Wq, 'bq': bq, 'Wk': Wk, 'bk': bk, 'Wv': Wv, 'bv': bv, 'Wo': Wo, 'norm_w': norm_w}
    _L0_attn_in = _L0_attn_setup()

    def _L0_ffn_setup():
        import jax, jax.numpy as jnp
        import numpy as np
        EPS_LN = 1e-05
        EPS_GATE = 1e-08

        def layer_norm(x, gamma, beta):
            mu = jnp.mean(x, axis=-1, keepdims=True)
            var = jnp.mean(jnp.square(x - mu), axis=-1, keepdims=True)
            return (x - mu) * jax.lax.rsqrt(var + EPS_LN) * gamma + beta
        key = jax.random.key(seed)
        ks = jax.random.split(key, 8)
        B, S, D, E, H = (4, 512, 128, 4, 256)
        s_in = 1.0 / np.sqrt(D)
        s_h = 1.0 / np.sqrt(H)
        return {'h': jax.random.normal(ks[0], (B, S, D), dtype=jnp.float32), 'router_w': jax.random.uniform(ks[1], (E, D), jnp.float32, -s_in, s_in), 'rn_g': jnp.ones((D,), jnp.float32), 'rn_b': jnp.zeros((D,), jnp.float32), 'w1': jax.random.uniform(ks[2], (E, D, H), jnp.float32, -s_in, s_in), 'ln_g': jnp.ones((E, H), jnp.float32), 'ln_b': jnp.zeros((E, H), jnp.float32), 'w2': jax.random.uniform(ks[3], (E, H, D), jnp.float32, -s_h, s_h), 'on_g': jnp.ones((D,), jnp.float32), 'on_b': jnp.zeros((D,), jnp.float32)}
    _L0_ffn_in = _L0_ffn_setup()
    _d = {'L0_attn_x': _L0_attn_in['x'], 'L0_attn_Wq': _L0_attn_in['Wq'], 'L0_attn_bq': _L0_attn_in['bq'], 'L0_attn_Wk': _L0_attn_in['Wk'], 'L0_attn_bk': _L0_attn_in['bk'], 'L0_attn_Wv': _L0_attn_in['Wv'], 'L0_attn_bv': _L0_attn_in['bv'], 'L0_attn_Wo': _L0_attn_in['Wo'], 'L0_attn_norm_w': _L0_attn_in['norm_w'], 'L0_ffn_router_w': _L0_ffn_in['router_w'], 'L0_ffn_rn_g': _L0_ffn_in['rn_g'], 'L0_ffn_rn_b': _L0_ffn_in['rn_b'], 'L0_ffn_w1': _L0_ffn_in['w1'], 'L0_ffn_ln_g': _L0_ffn_in['ln_g'], 'L0_ffn_ln_b': _L0_ffn_in['ln_b'], 'L0_ffn_w2': _L0_ffn_in['w2'], 'L0_ffn_on_g': _L0_ffn_in['on_g'], 'L0_ffn_on_b': _L0_ffn_in['on_b']}
    _x0 = _d['L0_attn_x']
    _d['L0_attn_x'] = jax.random.normal(jax.random.fold_in(jax.random.key(seed), 1), (32, 256, 128), dtype=_x0.dtype)
    del _x0
    return _d

def reference(L0_attn_x, L0_attn_Wq, L0_attn_bq, L0_attn_Wk, L0_attn_bk, L0_attn_Wv, L0_attn_bv, L0_attn_Wo, L0_attn_norm_w, L0_ffn_router_w, L0_ffn_rn_g, L0_ffn_rn_b, L0_ffn_w1, L0_ffn_ln_g, L0_ffn_ln_b, L0_ffn_w2, L0_ffn_on_g, L0_ffn_on_b):

    def _L0_attn_ref(x, Wq, bq, Wk, bk, Wv, bv, Wo, norm_w):
        import jax, jax.numpy as jnp
        import numpy as np
        D_MODEL = 128
        N_HEAD = 16
        D_HEAD = D_MODEL // N_HEAD
        N_CTX = 256
        ROPE_BASE = 10000.0
        SCALE = 1

        def _rope_cache(seq_len, d_head, dtype=jnp.float32):
            inv_freq = 1.0 / ROPE_BASE ** (jnp.arange(0, d_head, 2, dtype=jnp.float32) / d_head)
            t = jnp.arange(seq_len, dtype=jnp.float32)
            freqs = jnp.outer(t, inv_freq)
            emb = jnp.concatenate([freqs, freqs], -1)
            cos = jnp.cos(emb)[None, :, None, :].astype(dtype)
            sin = jnp.sin(emb)[None, :, None, :].astype(dtype)
            return (cos, sin)

        def _apply_rope(x, cos, sin):
            x_even = x[..., 0::2]
            x_odd = x[..., 1::2]
            x_rot = jnp.stack([-x_odd, x_even], axis=-1).reshape(x.shape)
            return x * cos + x_rot * sin

        def _rmsnorm(x, w):
            eps = jnp.finfo(x.dtype).eps
            var = jnp.mean(jnp.square(x), axis=-1, keepdims=True)
            return x * jax.lax.rsqrt(var + eps) * w
        B, S, _ = x.shape
        split = lambda t: t.reshape(B, S, N_HEAD, D_HEAD)
        q = split(x @ Wq.T + bq)
        k = split(x @ Wk.T + bk)
        v = split(x @ Wv.T + bv)
        cos, sin = _rope_cache(S, D_HEAD, x.dtype)
        q = _apply_rope(_rmsnorm(q, norm_w), cos, sin)
        k = _apply_rope(_rmsnorm(k, norm_w), cos, sin)
        scores = jnp.einsum('bqhd,bkhd->bhqk', q, k)
        causal = jnp.tril(jnp.ones((S, S), x.dtype))
        pattern = jnp.square(scores / D_HEAD) * causal
        z = jnp.einsum('bhqk,bkhd->bqhd', pattern, v).reshape(B, S, D_MODEL)
        return x + z @ Wo.T * SCALE

    def _L0_ffn_ref(h, router_w, rn_g, rn_b, w1, ln_g, ln_b, w2, on_g, on_b):
        import jax, jax.numpy as jnp
        import numpy as np
        EPS_LN = 1e-05
        EPS_GATE = 1e-08

        def layer_norm(x, gamma, beta):
            mu = jnp.mean(x, axis=-1, keepdims=True)
            var = jnp.mean(jnp.square(x - mu), axis=-1, keepdims=True)
            return (x - mu) * jax.lax.rsqrt(var + EPS_LN) * gamma + beta
        D = h.shape[-1]
        h_norm = layer_norm(h, rn_g, rn_b)
        g = jax.nn.softmax(jnp.einsum('bsd,ed->bse', h_norm, router_w), axis=-1)
        top2_w, top2_idx = jax.lax.top_k(g, 2)
        top2_w = top2_w / (jnp.sum(top2_w, axis=-1, keepdims=True) + EPS_GATE)
        hid = jnp.einsum('bsd,edh->bseh', h, w1)
        hid = jax.nn.relu(layer_norm(hid, ln_g, ln_b))
        expert_out = jnp.einsum('bseh,ehd->bsed', hid, w2)
        idx = jnp.broadcast_to(top2_idx[..., None], top2_idx.shape + (D,))
        top2_out = jnp.take_along_axis(expert_out, idx, axis=-2)
        out = jnp.sum(top2_out * top2_w[..., None], axis=-2)
        return layer_norm(out, on_g, on_b)
    x = L0_attn_x
    xn = _layernorm(x, axis=-1)
    x = x + _L0_attn_ref(xn, L0_attn_Wq, L0_attn_bq, L0_attn_Wk, L0_attn_bk, L0_attn_Wv, L0_attn_bv, L0_attn_Wo, L0_attn_norm_w) + _L0_ffn_ref(xn, L0_ffn_router_w, L0_ffn_rn_g, L0_ffn_rn_b, L0_ffn_w1, L0_ffn_ln_g, L0_ffn_ln_b, L0_ffn_w2, L0_ffn_on_g, L0_ffn_on_b)
    return x

_drawn_inputs = setup_inputs


def setup_inputs(seed=0):
    import zlib

    import numpy as np

    out = dict(_drawn_inputs(seed))
    spreads = {'L0_attn_norm_w': (1.0, 0.2),
     'L0_ffn_rn_g': (1.0, 0.2),
     'L0_ffn_rn_b': (0.0, 0.1),
     'L0_ffn_ln_g': (1.0, 0.2),
     'L0_ffn_ln_b': (0.0, 0.1),
     'L0_ffn_on_g': (1.0, 0.2),
     'L0_ffn_on_b': (0.0, 0.1)}
    factors = {'L0_attn_bq': 5.499, 'L0_attn_bk': 4.622}
    for name, (base, spread) in spreads.items():
        noise = np.random.default_rng([zlib.crc32(name.encode()), seed]).standard_normal(out[name].shape)
        drawn = base * np.exp(spread * noise) if base else spread * noise
        out[name] = jnp.asarray(drawn.astype(out[name].dtype))
    for name, factor in factors.items():
        out[name] = (out[name] * factor).astype(out[name].dtype)
    return out
```

```python
from contextlib import ExitStack

import numpy as np

import concourse.bass as bass
from concourse import mybir

F32 = mybir.dt.float32
F32R = mybir.dt.float32r
F16 = mybir.dt.float16
ALU = mybir.AluOpType
ACT = mybir.ActivationFunctionType
AX_X = mybir.AxisListType.X

B, SEQ, D = 32, 256, 128
NT = SEQ // 128
HEADS, DH = 16, 8
NG = 4
NC = HEADS // NG
EXPERTS, HID = 4, 256
CH = HID // 128
SLOTS = 4
QKV = 3 * D
PROJ = QKV + EXPERTS
EPS_LN = 1e-5
EPS_RMS = float(np.finfo(np.float32).eps)
EPS_GATE = 1e-8
QK_SCALE = 16.0


class Signal:

    def __init__(self, sem, per):
        self.sem, self.per = sem, per

    def at(self, j, n):
        return j * self.per + n

    def due(self, j, n):
        value = self.at(j, n)
        return not isinstance(value, int) or value > 0


def build(nc, x, wq, bq, wk, bk, wv, bv, wo, norm_w, router_w, rn_g, rn_b, w1, ln_g, ln_b, w2,
          on_g, on_b, ident_c, rope_c, earlier_c, out):
    ctx = ExitStack()
    with ctx:
        def sb(name, shape, dt=F32):
            return ctx.enter_context(nc.sbuf_tensor(name, shape, dt))

        def ps(name, shape):
            return ctx.enter_context(nc.psum_tensor(name, shape, F32))

        def signal(name, per):
            return Signal(ctx.enter_context(nc.semaphore(name)), per)

        ident = sb("ident", [128, 128])
        ident16 = sb("ident16", [128, 128], F16)
        rope = sb("rope", [128, 2, NT, DH])
        earlier = sb("earlier", [128, EXPERTS, EXPERTS])
        w_raw = sb("w_raw", [128, 4, D])
        bias_raw = sb("bias_raw", [128, 3, D])
        bias = sb("bias", [128, QKV])
        router_raw = sb("router_raw", [EXPERTS, D])
        rn_cols = sb("rn_cols", [128, 2])
        w1_raw = sb("w1_raw", [128, EXPERTS, HID])
        w1_c = sb("w1_c", [128, EXPERTS, HID])
        w1_g = sb("w1_g", [128, EXPERTS, HID])
        w1_mean = sb("w1_mean", [128, EXPERTS])
        w1_ct = sb("w1_ct", [128, EXPERTS * CH, D])
        ln_g_all = sb("ln_g_all", [128, EXPERTS, HID])
        b_raw = sb("b_raw", [128, EXPERTS * HID])
        w2_sb = sb("w2_sb", [128, EXPERTS * CH, D])
        on_gb = sb("on_gb", [128, 2, D])
        nw = sb("nw", [128, DH])
        nw_m = sb("nw_m", [128, 4])
        nw_s = sb("nw_s", [128, DH])
        proj_h = sb("proj_h", [128, PROJ], F32R)
        proj_l = sb("proj_l", [128, PROJ], F32R)
        router_t = sb("router_t", [128, EXPERTS])
        router_g = sb("router_g", [128, EXPERTS])
        rn_b_all = sb("rn_b_all", [128, 128])
        router_b = sb("router_b", [128, EXPERTS])
        wo_t = sb("wo_t", [128, D])
        w1_h = sb("w1_h", [128, EXPERTS * HID], F32R)
        w1_l = sb("w1_l", [128, EXPERTS * HID], F32R)
        gram_h = sb("gram_h", [128, EXPERTS * D], F32R)
        gram_l = sb("gram_l", [128, EXPERTS * D], F32R)
        b_rows = sb("b_rows", [128, EXPERTS * HID], F32R)
        cos_t = sb("cos_t", [128, NT, DH])
        sin_t = sb("sin_t", [128, NT, DH])

        x_in = [sb(f"x_in{p}", [128, NT, D]) for p in range(2)]
        xn = [sb(f"xn{p}", [128, NT, D]) for p in range(2)]
        xt_h = [sb(f"xt_h{p}", [128, SEQ], F32R) for p in range(2)]
        xt_l = [sb(f"xt_l{p}", [128, SEQ], F32R) for p in range(2)]
        vz = [sb(f"vz{p}", [128, NT, NG * 136]) for p in range(2)]
        q_t = [sb(f"q_t{p}", [128, NG, SEQ], F16) for p in range(2)]
        k_t = [sb(f"k_t{p}", [128, NG, SEQ], F16) for p in range(2)]
        std_t = [sb(f"std_t{p}", [128, SEQ], F32R) for p in range(2)]
        scale_e = [sb(f"scale_e{p}", [128, NT, EXPERTS]) for p in range(2)]
        stats = sb("stats", [128, NT, 6])
        mean_var = sb("mean_var", [128, NT, 2])
        ln_x = sb("ln_x", [128, NT])
        r_x = sb("r_x", [128, NT])
        nx1 = sb("nx1", [128, NT])
        nx2 = sb("nx2", [128, NT])
        rstd_x = sb("rstd_x", [128, NT])
        qk = sb("qk", [128, NT, 2 * D])
        logits0 = sb("logits0", [128, NT, EXPERTS])
        qk_sq = sb("qk_sq", [128, NT, 2 * D])
        ms_sum = sb("ms_sum", [128, NT * 2 * HEADS])
        ms = sb("ms", [128, NT * 2 * HEADS])
        ln_ms = sb("ln_ms", [128, NT * 2 * HEADS])
        r_ms = sb("r_ms", [128, NT * 2 * HEADS])
        nm1 = sb("nm1", [128, NT * 2 * HEADS])
        nm2 = sb("nm2", [128, NT * 2 * HEADS])
        rms = sb("rms", [128, NT * 2 * HEADS])
        qk_n = sb("qk_n", [128, NT * 2 * D])
        rope1 = sb("rope1", [128, NT * 2 * D])
        rope2 = sb("rope2", [128, NT * 2 * D])
        qk_r = sb("qk_r", [128, NT * 2 * D])
        stack = sb("stack", [128, NT, 2, HEADS, SLOTS, DH], F16)
        NV = NT * EXPERTS
        var_raw = sb("var_raw", [128, NV])
        scrap = sb("scrap", [128, 2, D])
        var = sb("var", [128, NV + NT])
        ln_v = sb("ln_v", [128, NV + NT])
        r_v = sb("r_v", [128, NV + NT])
        nv1 = sb("nv1", [128, NV + NT])
        nv2 = sb("nv2", [128, NV + NT])
        rstd_v = sb("rstd_v", [128, NV + NT])
        std = sb("std", [128, NV])
        std_cols = sb("std_cols", [128, NT, 96])
        rt1 = sb("rt1", [128, NT])
        lg1 = sb("lg1", [128, NT, EXPERTS])
        lg2 = sb("lg2", [128, NT, EXPERTS])
        lg_max = sb("lg_max", [128, NT])
        lg3 = sb("lg3", [128, NT, EXPERTS])
        gate = sb("gate", [128, NT, EXPERTS])
        gate_sum = sb("gate_sum", [128, NT])
        above = sb("above", [128, NT, EXPERTS, EXPERTS])
        equal = sb("equal", [128, NT, EXPERTS, EXPERTS])
        tied = sb("tied", [128, NT, EXPERTS, EXPERTS])
        beaten = sb("beaten", [128, NT, EXPERTS, EXPERTS])
        rank = sb("rank", [128, NV])
        chosen = sb("chosen", [128, NT, EXPERTS])
        chosen_sum = sb("chosen_sum", [128, NT])
        gate_den = sb("gate_den", [128, NT])
        gate_inv = sb("gate_inv", [128, NT])
        weight = sb("weight", [128, NT, EXPERTS])
        probs = [sb(f"probs{b}", [128, NC, 3 * 128]) for b in range(2)]
        hid_t = [sb(f"hid_t{b}", [128, CH * SEQ]) for b in range(2)]
        acc = sb("acc", [128, NT, D])
        z_t = sb("z_t", [128, SEQ])
        stats_f = sb("stats_f", [128, NT, 6])
        mean_var_f = sb("mean_var_f", [128, NT, 2])
        ln_f = sb("ln_f", [128, NT])
        r_f = sb("r_f", [128, NT])
        nf1 = sb("nf1", [128, NT])
        nf2 = sb("nf2", [128, NT])
        rstd_f = sb("rstd_f", [128, NT])
        ffn_n = sb("ffn_n", [128, NT, D])
        ffn_g = sb("ffn_g", [128, NT, D])
        base0 = sb("base0", [128, NT, D])
        base1 = sb("base1", [128, NT, D])
        base2 = sb("base2", [128, NT, D])
        eps_ln = sb("eps_ln", [128, 1])
        y = [sb(f"y{p}", [128, NT, D]) for p in range(2)]

        ps_s = ps("ps_s", [128, NC, 512])
        ps_z = ps("ps_z", [128, 512])
        ps_h = ps("ps_h", [128, 512])
        ps_o = ps("ps_o", [128, 512])
        ps_a = ps("ps_a", [128, 512])

        LOADS = 19
        loaded = signal("loaded", 16 * LOADS)
        b_loaded = signal("b_loaded", 16 * 3 * EXPERTS)
        v_chain = signal("v_chain", 1)
        eps_set = signal("eps_set", 1)
        zeroed = signal("zeroed", 1)
        v_setup = signal("v_setup", 1)
        p_setup = signal("p_setup", 1)
        x_loaded = [signal(f"x_loaded{p}", 16 // 2) for p in range(2)]
        y_stored = [signal(f"y_stored{p}", 16 // 2) for p in range(2)]
        s_stats = signal("s_stats", NT)
        s_mean_var = signal("s_mean_var", NT)
        s_ln_x = signal("s_ln_x", 1)
        s_r_x = signal("s_r_x", 1)
        s_newton_x = signal("s_newton_x", 3)
        s_xn = signal("s_xn", NT)
        s_xt = signal("s_xt", 1)
        s_xt_h = signal("s_xt_h", 1)
        s_xt_l = signal("s_xt_l", 1)
        s_proj = signal("s_proj", NT)
        s_qk = signal("s_qk", NT)
        s_v = signal("s_v", NT)
        s_logits0 = signal("s_logits0", NT)
        s_qk_sq = signal("s_qk_sq", 1)
        s_ms = signal("s_ms", 2)
        s_ln_ms = signal("s_ln_ms", 1)
        s_r_ms = signal("s_r_ms", 1)
        s_newton_ms = signal("s_newton_ms", 3)
        s_qk_n = signal("s_qk_n", 1)
        s_rope1 = signal("s_rope1", 1)
        s_rope2 = signal("s_rope2", 1)
        s_qk_r = signal("s_qk_r", 1)
        s_high = signal("s_high", 1)
        s_low = signal("s_low", 1)
        s_stack = signal("s_stack", 2)
        s_q_ps = signal("s_q_ps", 1)
        s_q_t = signal("s_q_t", 1)
        s_k_ps = signal("s_k_ps", 1)
        s_k_t = signal("s_k_t", 1)
        s_gram = signal("s_gram", NT)
        s_var_raw = signal("s_var_raw", NV)
        s_var = signal("s_var", 3)
        s_ln_v = signal("s_ln_v", 1)
        s_r_v = signal("s_r_v", 1)
        s_newton_v = signal("s_newton_v", 3)
        s_std = signal("s_std", 1)
        s_std_cols = signal("s_std_cols", 3)
        s_std_ps = signal("s_std_ps", 1)
        s_std_t = signal("s_std_t", 1)
        s_lg = signal("s_lg", 4)
        s_gate = signal("s_gate", 1)
        s_rank = signal("s_rank", 6)
        s_weight = signal("s_weight", 5)
        s_scale_e = signal("s_scale_e", 1)
        s_scores = signal("s_scores", 2 * NG)
        s_probs = signal("s_probs", 2 * NG)
        s_masked = signal("s_masked", 2 * NG)
        s_pv = signal("s_pv", NG)
        s_hid = signal("s_hid", NG)
        s_relu = [signal("s_relu_even", NG // 2), signal("s_relu_odd", NG // 2)]
        s_expert = signal("s_expert", NG)
        s_acc = signal("s_acc", NG * NT)
        s_z_t = signal("s_z_t", 1)
        s_attn = signal("s_attn", 1)
        s_base0 = signal("s_base0", 1)
        s_base1 = signal("s_base1", 1)
        s_base2 = signal("s_base2", 1)
        s_stats_f = signal("s_stats_f", NT)
        s_mean_var_f = signal("s_mean_var_f", NT)
        s_ln_f = signal("s_ln_f", 1)
        s_r_f = signal("s_r_f", 1)
        s_newton_f = signal("s_newton_f", 3)
        s_ffn_n = signal("s_ffn_n", NT)
        s_ffn_g = signal("s_ffn_g", 1)
        s_y = signal("s_y", 1)

        x_v = x.rearrange("b (t p) d -> p (b t) d", p=128)
        out_v = out.rearrange("b (t p) d -> p (b t) d", p=128)
        V_CENTRED, V_ROUTER_T, V_W1_CT, V_DONE = 1, 2, 3, 4
        P_WEIGHTS, P_W1_CT, P_GRAM, P_ROUTER_B = 1, 2, 3, 4

        block = ctx.enter_context(nc.Block())

        def batches(eng, batch, first, straight_after):
            for j in range(first, 2):
                batch(j, j % 2)
            with eng.Fori(1, B // 2 - 1) as i:
                for p in range(2):
                    batch(i * 2 + p, p)
            for j in range(B - 2, B + straight_after):
                batch(j, j % 2)

        def known(j):
            return isinstance(j, int)

        def exists(j):
            return not known(j) or 0 <= j < B

        @block.sync
        def _(sp):
            def load(dst, src):
                sp.dma_start(dst, src).then_inc(loaded.sem, 16)

            load(ident[:], ident_c)
            for n, w in enumerate((wq, wk, wv, wo)):
                load(w_raw[:, n, :], w)
            load(w1_raw[:], w1.rearrange("e d h -> d e h"))
            load(nw[:], norm_w.partition_broadcast(128))
            load(router_raw[:], router_w)
            load(rn_cols[:, 0:1], rn_g.unsqueeze(1))
            load(rn_cols[:, 1:2], rn_b.unsqueeze(1))
            load(rope[:], rope_c)
            load(earlier[:], earlier_c.partition_broadcast(128))
            for n, b in enumerate((bq, bk, bv)):
                load(bias_raw[:, n, :], b.partition_broadcast(128))
            load(ln_g_all[:], ln_g.partition_broadcast(128))
            load(w2_sb[:], w2.rearrange("e (c h) d -> h (e c) d", h=128))
            load(on_gb[:, 0, :], on_g.partition_broadcast(128))
            load(on_gb[:, 1, :], on_b.partition_broadcast(128))
            sp.wait_ge(zeroed.sem, 1)
            for quadrant in range(3):
                for e in range(EXPERTS):
                    r = 32 * quadrant + e
                    sp.dma_start(b_raw[r:r + 1, e * HID:(e + 1) * HID],
                                 ln_b[e:e + 1, :]).then_inc(b_loaded.sem, 16)

            def batch(j, p):
                n = j + 2
                if exists(n):
                    if s_base0.due(j, 1):
                        sp.wait_ge(s_base0.sem, s_base0.at(j, 1))
                    sp.dma_start(x_in[p][:], x_v[:, bass.ds(n * NT, NT), :]).then_inc(x_loaded[p].sem, 16)
                if exists(j - 1):
                    if s_y.due(j - 1, 1):
                        sp.wait_ge(s_y.sem, s_y.at(j - 1, 1))
                    sp.dma_start(out_v[:, bass.ds((j - 1) * NT, NT), :],
                                 y[1 - p][:]).then_inc(y_stored[1 - p].sem, 16)

            batches(sp, batch, -2, 1)
            for p in range(2):
                sp.wait_ge(y_stored[p].sem, y_stored[p].at(B - 2, 16))

        @block.vector
        def _(dve):
            v = nc.vector
            chain = [0]

            def link(ins):
                chain[0] += 1
                ins.then_inc(v_chain.sem, 1)
                dve.wait_ge(v_chain.sem, chain[0])

            def perm(ap):
                return ap.rearrange("p (c g d) -> p g c d", c=NC, g=NG)

            def rows(ap):
                return ap.rearrange("p (g c d) -> p g c d", c=NC, g=NG)

            def setup():
                v.memset(b_raw[:], 0.0).then_inc(zeroed.sem, 1)
                for p in range(2):
                    link(v.memset(vz[p][:], 0.0))
                    link(v.memset(std_t[p][:].bitcast(F32), 0.0))
                link(v.memset(std_cols[:], 0.0))
                dve.wait_ge(loaded.sem, 16 * LOADS)
                link(v.tensor_reduce(w1_mean[:], w1_raw[:], AX_X, ALU.add))
                link(v.tensor_scalar(w1_mean[:], w1_mean[:], 1.0 / HID, None, ALU.mult))
                v.tensor_tensor(w1_c[:], w1_raw[:], w1_mean[:].unsqueeze(2).to_broadcast([128, EXPERTS, HID]),
                                ALU.subtract).then_inc(v_setup.sem, 1)
                dve.wait_ge(v_setup.sem, V_CENTRED)
                link(v.tensor_copy(ident16[:], ident[:]))
                link(v.tensor_reduce(nw_m[:, 0:1], nw[:], AX_X, ALU.max, apply_absolute_value=True))
                link(v.tensor_scalar(nw_m[:, 0:1], nw_m[:, 0:1], 1e-30, None, ALU.max))
                link(v.reciprocal(nw_m[:, 1:2], nw_m[:, 0:1]))
                link(v.tensor_tensor(nw_m[:, 2:3], nw_m[:, 0:1], nw_m[:, 0:1], ALU.mult))
                link(v.tensor_tensor(nw_m[:, 3:4], nw_m[:, 2:3], nw_m[:, 2:3], ALU.mult))
                link(v.tensor_scalar(nw_s[:], nw[:], nw_m[:, 1:2], QK_SCALE, ALU.mult, ALU.mult))
                link(v.tensor_tensor(cos_t[:], rope[:, 0], nw_s[:].unsqueeze(1).to_broadcast([128, NT, DH]),
                                     ALU.mult))
                nw_pairs = nw_s[:].rearrange("p (a two) -> p a two", two=2)
                for t in range(NT):
                    link(v.tensor_tensor(sin_t[:, t].rearrange("p (a two) -> p a two", two=2),
                                         rope[:, 1, t].rearrange("p (a two) -> p a two", two=2),
                                         nw_pairs[:, :, ::-1], ALU.mult))
                link(v.tensor_tensor(w1_g[:], w1_c[:], ln_g_all[:], ALU.mult))
                link(v.tensor_copy(w1_h[:], w1_g[:].rearrange("p e h -> p (e h)")))
                link(v.tensor_tensor(w1_l[:], w1_g[:].rearrange("p e h -> p (e h)"),
                                     w1_h[:].bitcast(F32), ALU.subtract))
                for n in range(2):
                    link(v.tensor_copy(rows(bias[:, n * D:(n + 1) * D]), perm(bias_raw[:, n, :])))
                link(v.tensor_copy(bias[:, 2 * D:QKV], bias_raw[:, 2, :]))
                link(v.tensor_copy(rn_b_all[:], rn_cols[:, 1:2].to_broadcast([128, 128])))
                dve.wait_ge(b_loaded.sem, 16 * 3 * EXPERTS)
                link(v.tensor_copy(b_rows[:], b_raw[:]))
                link(v.tensor_tensor(b_rows[64:96, :], b_raw[64:96, :],
                                     b_rows[64:96, :].bitcast(F32), ALU.subtract))
                dve.wait_ge(p_setup.sem, P_WEIGHTS)
                for n in range(2):
                    w_t = ps_s[:, 0, n * D:(n + 1) * D]
                    link(v.tensor_copy(rows(proj_h[:, n * D:(n + 1) * D]), perm(w_t)))
                    link(v.tensor_tensor(rows(proj_l[:, n * D:(n + 1) * D]), perm(w_t),
                                         rows(proj_h[:, n * D:(n + 1) * D]).bitcast(F32), ALU.subtract))
                w_t = ps_s[:, 0, 2 * D:3 * D]
                link(v.tensor_copy(proj_h[:, 2 * D:QKV], w_t))
                link(v.tensor_tensor(proj_l[:, 2 * D:QKV], w_t, proj_h[:, 2 * D:QKV].bitcast(F32), ALU.subtract))
                link(v.tensor_scalar(wo_t[:], ps_s[:, 0, 3 * D:4 * D], nw_m[:, 3:4], None, ALU.mult))
                v.tensor_copy(router_t[:], ps_s[:, 1, 0:EXPERTS]).then_inc(v_setup.sem, 1)
                dve.wait_ge(v_setup.sem, V_ROUTER_T)
                link(v.tensor_scalar(router_g[:], router_t[:], rn_cols[:, 0:1], None, ALU.mult))
                link(v.tensor_copy(proj_h[:, QKV:PROJ], router_g[:]))
                link(v.tensor_tensor(proj_l[:, QKV:PROJ], router_g[:], proj_h[:, QKV:PROJ].bitcast(F32),
                                     ALU.subtract))
                dve.wait_ge(p_setup.sem, P_W1_CT)
                v.tensor_copy(w1_ct[:].rearrange("p c d -> p (c d)"),
                              ps_s[:, 2:4, :].rearrange("p b n -> p (b n)")).then_inc(v_setup.sem, 1)
                dve.wait_ge(p_setup.sem, P_GRAM)
                link(v.tensor_scalar(gram_h[:], ps_h[:], 1.0 / HID, None, ALU.mult))
                link(v.scalar_tensor_tensor(gram_l[:], ps_h[:], 1.0 / HID, gram_h[:].bitcast(F32),
                                            ALU.mult, ALU.subtract))
                dve.wait_ge(p_setup.sem, P_ROUTER_B)
                v.tensor_copy(router_b[:], ps_o[:, 0:EXPERTS]).then_inc(v_setup.sem, 1)

            def newton(s, j, value, guess, t1, t2, result):
                v.scalar_tensor_tensor(t1, guess, -0.5, guess, ALU.mult, ALU.mult).then_inc(s.sem, 1)
                dve.wait_ge(s.sem, s.at(j, 1))
                v.scalar_tensor_tensor(t2, value[0], value[1], t1, ALU.add, ALU.mult).then_inc(s.sem, 1)
                dve.wait_ge(s.sem, s.at(j, 2))
                v.scalar_tensor_tensor(result, t2, 1.5, guess, ALU.add, ALU.mult).then_inc(s.sem, 1)

            def input_stats(n, p):
                dve.wait_ge(x_loaded[p].sem, x_loaded[p].at(n - p, 16))
                for t in range(NT):
                    v.bn_stats(stats[:, t, :], x_in[p][:, t, :]).then_inc(s_stats.sem, 1)
                for t in range(NT):
                    dve.wait_ge(s_stats.sem, s_stats.at(n, t + 1))
                    dve.nop(nofuse=True)
                    v.bn_aggr(mean_var[:, t, :], stats[:, t, :]).then_inc(s_mean_var.sem, 1)

            def input_norm(n, p):
                dve.wait_ge(s_r_x.sem, s_r_x.at(n, 1))
                newton(s_newton_x, n, (mean_var[:, :, 1], EPS_LN), r_x[:], nx1[:], nx2[:], rstd_x[:])
                dve.wait_ge(s_newton_x.sem, s_newton_x.at(n, 3))
                if s_base0.due(n - 2, 1):
                    dve.wait_ge(s_base0.sem, s_base0.at(n - 2, 1))
                for t in range(NT):
                    v.tensor_scalar(xn[p][:, t, :], x_in[p][:, t, :], mean_var[:, t, 0:1], rstd_x[:, t:t + 1],
                                    ALU.subtract, ALU.mult).then_inc(s_xn.sem, 1)

            def xt_low(n, p):
                dve.wait_ge(s_xt_h.sem, s_xt_h.at(n, 1))
                if s_hid.due(n - 2, NG):
                    dve.wait_ge(s_hid.sem, s_hid.at(n - 2, NG))
                v.tensor_tensor(xt_l[p][:], ps_a[:, 0:SEQ], xt_h[p][:].bitcast(F32),
                                ALU.subtract).then_inc(s_xt_l.sem, 1)

            def take_projections(n, p, t):
                dve.wait_ge(s_proj.sem, s_proj.at(n, t + 1))
                v.tensor_tensor(qk[:, t, :], ps_a[:, 0:2 * D], bias[:, 0:2 * D], ALU.add).then_inc(s_qk.sem, 1)
                if s_pv.due(n - 2, NG):
                    dve.wait_ge(s_pv.sem, s_pv.at(n - 2, NG))
                v_blocks = vz[p][:, t, :].rearrange("p (g s) -> p g s", g=NG)[:, :, 0:NC * 32]
                v_blocks = v_blocks.rearrange("p g (c s) -> p g c s", c=NC)[:, :, :, 0:DH]
                v.tensor_tensor(v_blocks, perm(ps_a[:, 2 * D:QKV]), perm(bias[:, 2 * D:QKV]),
                                ALU.add).then_inc(s_v.sem, 1)
                v.tensor_copy(logits0[:, t, :], ps_a[:, QKV:PROJ]).then_inc(s_logits0.sem, 1)

            def mean_squares(n):
                dve.wait_ge(s_qk_sq.sem, s_qk_sq.at(n, 1))
                v.tensor_reduce(ms_sum[:], qk_sq[:].rearrange("p t (h d) -> p (t h) d", d=DH), AX_X,
                                ALU.add).then_inc(s_ms.sem, 1)
                dve.wait_ge(s_ms.sem, s_ms.at(n, 1))
                v.tensor_scalar(ms[:], ms_sum[:], 1.0 / DH, EPS_RMS, ALU.mult, ALU.add).then_inc(s_ms.sem, 1)

            def rms_norm(n):
                dve.wait_ge(s_r_ms.sem, s_r_ms.at(n, 1))
                newton(s_newton_ms, n, (ms[:], 0.0), r_ms[:], nm1[:], nm2[:], rms[:])
                dve.wait_ge(s_newton_ms.sem, s_newton_ms.at(n, 3))
                v.tensor_tensor(qk_n[:].rearrange("p (h d) -> p h d", d=DH),
                                qk[:].rearrange("p t (h d) -> p (t h) d", d=DH),
                                rms[:].unsqueeze(2).to_broadcast([128, NT * 2 * HEADS, DH]),
                                ALU.mult).then_inc(s_qk_n.sem, 1)

            def rope_cos(n):
                dve.wait_ge(s_qk_n.sem, s_qk_n.at(n, 1))
                v.tensor_tensor(rope1[:].rearrange("p (t h d) -> p t h d", t=NT, d=DH),
                                qk_n[:].rearrange("p (t h d) -> p t h d", t=NT, d=DH),
                                cos_t[:].unsqueeze(2).to_broadcast([128, NT, 2 * HEADS, DH]),
                                ALU.mult).then_inc(s_rope1.sem, 1)

            def rope_sum(n):
                dve.wait_ge(s_rope1.sem, s_rope1.at(n, 1))
                dve.wait_ge(s_rope2.sem, s_rope2.at(n, 1))
                v.tensor_tensor(qk_r[:], rope1[:], rope2[:], ALU.add).then_inc(s_qk_r.sem, 1)

            def stack_low(n):
                dve.wait_ge(s_high.sem, s_high.at(n, 1))
                high_low = stack[:].rearrange("p t k h s d -> p (t k h) s d")
                v.tensor_tensor(high_low[:, :, 1, :], qk_r[:].rearrange("p (h d) -> p h d", d=DH),
                                high_low[:, :, 0, :], ALU.subtract).then_inc(s_low.sem, 1)
                dve.wait_ge(s_low.sem, s_low.at(n, 1))
                k_rows, q_rows = stack[:, :, 1], stack[:, :, 0]
                v.tensor_copy(k_rows[:, :, :, 2:4, :].rearrange("p t h s d -> p t h (s d)"),
                              k_rows[:, :, :, 0:2, :].rearrange("p t h s d -> p t h (s d)")).then_inc(s_stack.sem, 1)
                for t in range(NT):
                    ins = v.tensor_copy(q_rows[:, t, :, 2:4, :], q_rows[:, t, :, 1::-1, :])
                    if t == NT - 1:
                        ins.then_inc(s_stack.sem, 1)

            def take_q(n, p):
                dve.wait_ge(s_q_ps.sem, s_q_ps.at(n, 1))
                if s_scores.due(n - 2, 2 * NG):
                    dve.wait_ge(s_scores.sem, s_scores.at(n - 2, 2 * NG))
                v.tensor_copy(q_t[p][:].rearrange("p g s -> p (g s)"),
                              ps_a[:].bitcast(F16)).then_inc(s_q_t.sem, 1)

            def variances(n, p, t):
                dve.wait_ge(s_gram.sem, s_gram.at(n, t + 1))
                for e in range(EXPERTS):
                    k = t * EXPERTS + e
                    v.tensor_tensor_reduce(out=scrap[:, k % 2, :], in0=ps_a[:, e * D:(e + 1) * D],
                                           in1=xn[p][:, t, :], scale=1.0, scalar=0.0, op0=ALU.mult,
                                           op1=ALU.add, accum_out=var_raw[:, k:k + 1]).then_inc(s_var_raw.sem, 1)
                    dve.wait_ge(s_var_raw.sem, s_var_raw.at(n, k + 1))

            def router_var(n):
                v.tensor_tensor(rt1[:], mean_var[:, :, 1], rstd_x[:], ALU.mult).then_inc(s_var.sem, 1)
                dve.wait_ge(s_var.sem, s_var.at(n, 1))
                v.tensor_tensor(var[:, NV:], rt1[:], rstd_x[:], ALU.mult).then_inc(s_var.sem, 1)

            def expert_var(n):
                v.tensor_copy(var[:, 0:NV], var_raw[:]).then_inc(s_var.sem, 1)

            def hidden_std(n):
                dve.wait_ge(s_r_v.sem, s_r_v.at(n, 1))
                newton(s_newton_v, n, (var[:], EPS_LN), r_v[:], nv1[:], nv2[:], rstd_v[:])
                dve.wait_ge(s_newton_v.sem, s_newton_v.at(n, 3))
                v.scalar_tensor_tensor(std[:], var[:, 0:NV], EPS_LN, rstd_v[:, 0:NV], ALU.add,
                                       ALU.mult).then_inc(s_std.sem, 1)
                dve.wait_ge(s_std.sem, s_std.at(n, 1))
                if s_std_ps.due(n - 1, 1):
                    dve.wait_ge(s_std_ps.sem, s_std_ps.at(n - 1, 1))
                std3 = std[:].rearrange("p (t e) -> p t e", t=NT)
                high = std_cols[:, :, 0:EXPERTS]
                v.tensor_copy(high.bitcast(F32R), std3).then_inc(s_std_cols.sem, 1)
                dve.wait_ge(s_std_cols.sem, s_std_cols.at(n, 1))
                v.tensor_tensor(std_cols[:, :, 32:32 + EXPERTS], std3, high, ALU.subtract).then_inc(s_std_cols.sem, 1)
                v.tensor_copy(std_cols[:, :, 64:64 + EXPERTS], high).then_inc(s_std_cols.sem, 1)

            def router_logits(n):
                both = [128, NT, EXPERTS]
                v.tensor_tensor(lg1[:], logits0[:], rstd_v[:, NV:].unsqueeze(2).to_broadcast(both),
                                ALU.mult).then_inc(s_lg.sem, 1)
                dve.wait_ge(s_lg.sem, s_lg.at(n, 1))
                v.tensor_tensor(lg2[:], lg1[:], router_b[:].unsqueeze(1).to_broadcast(both),
                                ALU.add).then_inc(s_lg.sem, 1)
                dve.wait_ge(s_lg.sem, s_lg.at(n, 2))
                v.tensor_reduce(lg_max[:], lg2[:], AX_X, ALU.max).then_inc(s_lg.sem, 1)
                dve.wait_ge(s_lg.sem, s_lg.at(n, 3))
                v.tensor_tensor(lg3[:], lg2[:], lg_max[:].unsqueeze(2).to_broadcast(both),
                                ALU.subtract).then_inc(s_lg.sem, 1)

            def router_weights(n, p):
                both, square = [128, NT, EXPERTS], [128, NT, EXPERTS, EXPERTS]
                dve.wait_ge(s_gate.sem, s_gate.at(n, 1))
                g_j = gate[:].unsqueeze(2).to_broadcast(square)
                g_i = gate[:].unsqueeze(3).to_broadcast(square)
                v.tensor_tensor(above[:], g_j, g_i, ALU.is_gt).then_inc(s_rank.sem, 1)
                v.tensor_tensor(equal[:], g_j, g_i, ALU.is_equal).then_inc(s_rank.sem, 1)
                v.tensor_reduce(gate_sum[:], gate[:], AX_X, ALU.add).then_inc(s_rank.sem, 1)
                dve.wait_ge(s_rank.sem, s_rank.at(n, 2))
                v.tensor_tensor(tied[:], equal[:], earlier[:].unsqueeze(1).to_broadcast(square),
                                ALU.mult).then_inc(s_rank.sem, 1)
                dve.wait_ge(s_rank.sem, s_rank.at(n, 4))
                v.tensor_tensor(beaten[:], above[:], tied[:], ALU.add).then_inc(s_rank.sem, 1)
                dve.wait_ge(s_rank.sem, s_rank.at(n, 5))
                v.tensor_reduce(rank[:], beaten[:].rearrange("p t i j -> p (t i) j"), AX_X,
                                ALU.add).then_inc(s_rank.sem, 1)
                dve.wait_ge(s_rank.sem, s_rank.at(n, 6))
                v.scalar_tensor_tensor(chosen[:].rearrange("p t e -> p (t e)"), rank[:], 2.0,
                                       gate[:].rearrange("p t e -> p (t e)"), ALU.is_lt,
                                       ALU.mult).then_inc(s_weight.sem, 1)
                dve.wait_ge(s_weight.sem, s_weight.at(n, 1))
                v.tensor_reduce(chosen_sum[:], chosen[:], AX_X, ALU.add).then_inc(s_weight.sem, 1)
                dve.wait_ge(s_weight.sem, s_weight.at(n, 2))
                v.scalar_tensor_tensor(gate_den[:], gate_sum[:], EPS_GATE, chosen_sum[:], ALU.mult,
                                       ALU.add).then_inc(s_weight.sem, 1)
                dve.wait_ge(s_weight.sem, s_weight.at(n, 3))
                v.reciprocal(gate_inv[:], gate_den[:]).then_inc(s_weight.sem, 1)
                dve.wait_ge(s_weight.sem, s_weight.at(n, 4))
                v.tensor_tensor(weight[:], chosen[:], gate_inv[:].unsqueeze(2).to_broadcast(both),
                                ALU.mult).then_inc(s_weight.sem, 1)
                dve.wait_ge(s_weight.sem, s_weight.at(n, 5))
                v.tensor_tensor(scale_e[p][:].rearrange("p t e -> p (t e)"),
                                weight[:].rearrange("p t e -> p (t e)"), rstd_v[:, 0:NV],
                                ALU.mult).then_inc(s_scale_e.sem, 1)

            def relu_odd(j, e):
                dve.wait_ge(s_hid.sem, s_hid.at(j, e + 1))
                if s_expert.due(j, e - 1):
                    dve.wait_ge(s_expert.sem, s_expert.at(j, e - 1))
                v.tensor_scalar(hid_t[1][:], ps_h[:], 0.0, None, ALU.max).then_inc(s_relu[1].sem, 1)

            def combine(j, p, e):
                if e == 0:
                    dve.wait_ge(s_expert.sem, s_expert.at(j, 1))
                    dve.wait_ge(s_scale_e.sem, s_scale_e.at(j, 1))
                    if s_ffn_n.due(j - 1, NT):
                        dve.wait_ge(s_ffn_n.sem, s_ffn_n.at(j - 1, NT))
                elif e == EXPERTS - 1:
                    dve.wait_ge(s_attn.sem, s_attn.at(j, 1))
                else:
                    dve.wait_ge(s_expert.sem, s_expert.at(j, e + 1))
                for t in range(NT):
                    o = ps_o[:, t * D:(t + 1) * D]
                    s = scale_e[p][:, t, e:e + 1]
                    if e == 0:
                        v.tensor_scalar(acc[:, t, :], o, s, None, ALU.mult).then_inc(s_acc.sem, 1)
                    else:
                        dve.wait_ge(s_acc.sem, s_acc.at(j, e * NT - NT + t + 1))
                        v.scalar_tensor_tensor(acc[:, t, :], o, s, acc[:, t, :], ALU.mult,
                                               ALU.add).then_inc(s_acc.sem, 1)

            def add_attention(j):
                dve.wait_ge(s_base1.sem, s_base1.at(j, 1))
                if s_y.due(j - 1, 1):
                    dve.wait_ge(s_y.sem, s_y.at(j - 1, 1))
                v.tensor_tensor(base2[:].rearrange("p t d -> p (t d)"), ps_o[:, NT * D:2 * NT * D],
                                base1[:].rearrange("p t d -> p (t d)"), ALU.add).then_inc(s_base2.sem, 1)

            def output_stats(j):
                for t in range(NT):
                    dve.wait_ge(s_acc.sem, s_acc.at(j, (EXPERTS - 1) * NT + t + 1))
                    v.bn_stats(stats_f[:, t, :], acc[:, t, :]).then_inc(s_stats_f.sem, 1)
                for t in range(NT):
                    dve.wait_ge(s_stats_f.sem, s_stats_f.at(j, t + 1))
                    dve.nop(nofuse=True)
                    v.bn_aggr(mean_var_f[:, t, :], stats_f[:, t, :]).then_inc(s_mean_var_f.sem, 1)

            def output_norm(j):
                dve.wait_ge(s_r_f.sem, s_r_f.at(j, 1))
                newton(s_newton_f, j, (mean_var_f[:, :, 1], EPS_LN), r_f[:], nf1[:], nf2[:], rstd_f[:])
                dve.wait_ge(s_newton_f.sem, s_newton_f.at(j, 3))
                if s_ffn_g.due(j - 1, 1):
                    dve.wait_ge(s_ffn_g.sem, s_ffn_g.at(j - 1, 1))
                for t in range(NT):
                    v.tensor_scalar(ffn_n[:, t, :], acc[:, t, :], mean_var_f[:, t, 0:1], rstd_f[:, t:t + 1],
                                    ALU.subtract, ALU.mult).then_inc(s_ffn_n.sem, 1)

            def batch(j, p):
                n, n2 = j + 1, j + 2
                if exists(j - 1):
                    combine(j - 1, 1 - p, 3)
                    add_attention(j - 1)
                    output_stats(j - 1)
                if exists(n):
                    take_projections(n, 1 - p, 0)
                if exists(j):
                    relu_odd(j, 1)
                if exists(n):
                    take_projections(n, 1 - p, 1)
                    router_var(n)
                if exists(j - 1):
                    output_norm(j - 1)
                if exists(n):
                    variances(n, 1 - p, 0)
                if exists(n):
                    mean_squares(n)
                    variances(n, 1 - p, 1)
                    expert_var(n)
                if exists(j):
                    combine(j, p, 0)
                if exists(n):
                    rms_norm(n)
                    rope_cos(n)
                    hidden_std(n)
                    router_logits(n)
                    rope_sum(n)
                if exists(j):
                    relu_odd(j, 3)
                if exists(n):
                    stack_low(n)
                if exists(j):
                    combine(j, p, 1)
                if exists(n):
                    router_weights(n, 1 - p)
                    take_q(n, 1 - p)
                if exists(n2):
                    input_stats(n2, p)
                if exists(j):
                    combine(j, p, 2)
                if exists(n2):
                    input_norm(n2, p)
                    xt_low(n2, p)

            setup()
            batches(dve, batch, -2, 1)

        @block.scalar
        def _(act):
            a = nc.scalar
            a.preload_act_table_set("natural_log_exp_and_others")

            def inverse_root(first, second, j, result, log, value, eps):
                a.activation(log, value, ACT.Ln, bias=eps).then_inc(first.sem, 1)
                act.wait_ge(first.sem, first.at(j, 1))
                a.activation(result, log, ACT.Exp, scale=-0.5).then_inc(second.sem, 1)

            def input_root(n):
                act.wait_ge(s_mean_var.sem, s_mean_var.at(n, NT))
                inverse_root(s_ln_x, s_r_x, n, r_x[:], ln_x[:], mean_var[:, :, 1], eps_ln[:])

            def xt_high(n, p):
                act.wait_ge(s_xt.sem, s_xt.at(n, 1))
                if s_hid.due(n - 2, NG):
                    act.wait_ge(s_hid.sem, s_hid.at(n - 2, NG))
                a.activation(xt_h[p][:], ps_a[:, 0:SEQ], ACT.Copy).then_inc(s_xt_h.sem, 1)

            def squares(n):
                act.wait_ge(s_qk.sem, s_qk.at(n, NT))
                a.activation(qk_sq[:], qk[:], ACT.Square).then_inc(s_qk_sq.sem, 1)

            def rms_root(n):
                act.wait_ge(s_ms.sem, s_ms.at(n, 2))
                inverse_root(s_ln_ms, s_r_ms, n, r_ms[:], ln_ms[:], ms[:], 0.0)

            def expert_root(n):
                act.wait_ge(s_var.sem, s_var.at(n, 3))
                inverse_root(s_ln_v, s_r_v, n, r_v[:], ln_v[:], var[:], eps_ln[:])

            def high_half(n):
                act.wait_ge(s_qk_r.sem, s_qk_r.at(n, 1))
                a.activation(stack[:].rearrange("p t k h s d -> p (t k h) s d")[:, :, 0, :],
                             qk_r[:].rearrange("p (h d) -> p h d", d=DH), ACT.Copy).then_inc(s_high.sem, 1)

            def take_std(n, p):
                act.wait_ge(s_std_ps.sem, s_std_ps.at(n, 1))
                if s_hid.due(n - 2, NG):
                    act.wait_ge(s_hid.sem, s_hid.at(n - 2, NG))
                a.activation(std_t[p][0:96, :], ps_a[0:96, 0:SEQ], ACT.Copy).then_inc(s_std_t.sem, 1)

            def gates(n):
                act.wait_ge(s_lg.sem, s_lg.at(n, 4))
                a.activation(gate[:], lg3[:], ACT.Exp).then_inc(s_gate.sem, 1)

            def take_k(n, p):
                act.wait_ge(s_k_ps.sem, s_k_ps.at(n, 1))
                if s_scores.due(n - 2, 2 * NG):
                    act.wait_ge(s_scores.sem, s_scores.at(n - 2, 2 * NG))
                a.activation(k_t[p][:].rearrange("p g s -> p (g s)"), ps_a[:].bitcast(F16),
                             ACT.Copy).then_inc(s_k_t.sem, 1)

            def square_scores(j, g):
                for half in range(2):
                    act.wait_ge(s_scores.sem, s_scores.at(j, 2 * g + half + 1))
                    if half == 0:
                        if s_pv.due(j, g - 1):
                            act.wait_ge(s_pv.sem, s_pv.at(j, g - 1))
                    heads = slice(2 * half, 2 * half + 2)
                    a.activation(probs[g % 2][:, heads, :], ps_s[:, heads, 0:3 * 128], ACT.Square,
                                 scale=1.0 / (DH * QK_SCALE * QK_SCALE)).then_inc(s_probs.sem, 1)

            def relu_even(j, e):
                act.wait_ge(s_hid.sem, s_hid.at(j, e + 1))
                if s_expert.due(j, e - 1):
                    act.wait_ge(s_expert.sem, s_expert.at(j, e - 1))
                a.activation(hid_t[0][:], ps_h[:], ACT.Relu).then_inc(s_relu[0].sem, 1)

            def take_z(j):
                act.wait_ge(s_pv.sem, s_pv.at(j, NG))
                if s_attn.due(j - 1, 1):
                    act.wait_ge(s_attn.sem, s_attn.at(j - 1, 1))
                a.activation(z_t[:], ps_z[:, 0:SEQ], ACT.Copy).then_inc(s_z_t.sem, 1)

            def output_root(j):
                act.wait_ge(s_mean_var_f.sem, s_mean_var_f.at(j, NT))
                inverse_root(s_ln_f, s_r_f, j, r_f[:], ln_f[:], mean_var_f[:, :, 1], eps_ln[:])

            def batch(j, p):
                n, n2 = j + 1, j + 2
                if exists(j):
                    square_scores(j, 1)
                if exists(j - 1):
                    output_root(j - 1)
                if exists(n):
                    squares(n)
                if exists(j):
                    relu_even(j, 2)
                    square_scores(j, 2)
                if exists(n):
                    rms_root(n)
                    expert_root(n)
                if exists(n):
                    gates(n)
                    high_half(n)
                if exists(j):
                    square_scores(j, 3)
                if exists(n):
                    take_std(n, 1 - p)
                    take_k(n, 1 - p)
                if exists(n2):
                    input_root(n2)
                if exists(n):
                    relu_even(n, 0)
                    square_scores(n, 0)
                if exists(j):
                    take_z(j)
                if exists(n2):
                    xt_high(n2, p)

            act.wait_ge(eps_set.sem, 1)
            batches(act, batch, -2, 0)
            output_root(B - 1)

        @block.gpsimd
        def _(pool):
            g_ = nc.gpsimd

            def mask(j, g):
                for half in range(2):
                    pool.wait_ge(s_probs.sem, s_probs.at(j, 2 * g + half + 1))
                    pool.nop(nofuse=True)
                    heads = slice(2 * half, 2 * half + 2)
                    diagonal = probs[g % 2][:, heads, 0:2 * 128]
                    g_.affine_select(out=diagonal, in_=diagonal, compare_op=ALU.is_ge, fill=0.0, base=0,
                                     pattern=[[0, 2], [0, 2], [1, 128]],
                                     channel_multiplier=-1).then_inc(s_masked.sem, 1)

            def rope_sin(n):
                pool.wait_ge(s_qk_n.sem, s_qk_n.at(n, 1))
                pairs = "p (t h a two) -> p t h a two"
                g_.tensor_tensor(rope2[:].rearrange(pairs, t=NT, a=DH // 2, two=2),
                                 qk_n[:].rearrange(pairs, t=NT, a=DH // 2, two=2)[:, :, :, :, ::-1],
                                 sin_t[:].rearrange("p t (a two) -> p t a two", two=2).unsqueeze(2)
                                 .to_broadcast([128, NT, 2 * HEADS, DH // 2, 2]),
                                 ALU.mult).then_inc(s_rope2.sem, 1)

            def residual(j, p):
                pool.wait_ge(s_xn.sem, s_xn.at(j, NT))
                g_.tensor_tensor(base0[:], x_in[p][:], xn[p][:], ALU.add).then_inc(s_base0.sem, 1)
                pool.wait_ge(s_base0.sem, s_base0.at(j, 1))
                if s_base2.due(j - 1, 1):
                    pool.wait_ge(s_base2.sem, s_base2.at(j - 1, 1))
                g_.tensor_tensor(base1[:], base0[:], on_gb[:, 1:2, :].to_broadcast([128, NT, D]),
                                 ALU.add).then_inc(s_base1.sem, 1)

            def finish(j, p):
                pool.wait_ge(s_ffn_n.sem, s_ffn_n.at(j, NT))
                g_.tensor_tensor(ffn_g[:], ffn_n[:], on_gb[:, 0:1, :].to_broadcast([128, NT, D]),
                                 ALU.mult).then_inc(s_ffn_g.sem, 1)
                pool.wait_ge(s_ffn_g.sem, s_ffn_g.at(j, 1))
                pool.wait_ge(s_base2.sem, s_base2.at(j, 1))
                if y_stored[p].due(j - 2 - p, 16):
                    pool.wait_ge(y_stored[p].sem, y_stored[p].at(j - 2 - p, 16))
                g_.tensor_tensor(y[p][:], ffn_g[:], base2[:], ALU.add).then_inc(s_y.sem, 1)

            def batch(j, p):
                n = j + 1
                if exists(j):
                    mask(j, 1)
                if exists(j - 1):
                    finish(j - 1, 1 - p)
                if exists(j):
                    mask(j, 2)
                if exists(n):
                    rope_sin(n)
                if exists(j):
                    residual(j, p)
                    mask(j, 3)
                if exists(n):
                    mask(n, 0)

            pool.wait_ge(loaded.sem, 16 * LOADS)
            g_.memset(eps_ln[:], EPS_LN).then_inc(eps_set.sem, 1)
            batches(pool, batch, -1, 0)
            finish(B - 1, (B - 1) % 2)

        @block.tensor
        def _(pe):
            t_ = nc.tensor

            def setup():
                pe.wait_ge(loaded.sem, 16 * LOADS)
                for n in range(4):
                    t_.transpose(ps_s[:, 0, n * D:(n + 1) * D], w_raw[:, n, :], ident[:])
                t_.transpose(ps_s[:, 1, 0:EXPERTS], router_raw[:],
                             ident[0:EXPERTS, 0:EXPERTS]).then_inc(p_setup.sem, 1)
                pe.wait_ge(v_setup.sem, V_CENTRED)
                for c in range(EXPERTS * CH):
                    last = t_.transpose(ps_s[:, 2 + c // 4, (c % 4) * D:(c % 4 + 1) * D],
                                        w1_c[:].rearrange("p e h -> p (e h)")[:, c * 128:(c + 1) * 128], ident[:])
                last.then_inc(p_setup.sem, 1)
                pe.wait_ge(v_setup.sem, V_W1_CT)
                for e in range(EXPERTS):
                    for c in range(CH):
                        w_t = w1_ct[:, e * CH + c, :]
                        last = t_.matmul(ps_h[:, e * D:(e + 1) * D], w_t, w_t, start=(c == 0), stop=(c == CH - 1))
                last.then_inc(p_setup.sem, 1)
                t_.matmul(ps_o[:, 0:EXPERTS], rn_b_all[:], router_t[:], start=True,
                          stop=True).then_inc(p_setup.sem, 1)
                pe.wait_ge(v_setup.sem, V_DONE)

            def three_passes(dst, stationary, moving, start=True, stop=True):
                (sh, sl), (mh, ml) = stationary, moving
                t_.matmul(dst, sh, mh, start=start, stop=False)
                t_.matmul(dst, sh, ml, start=False, stop=False)
                return t_.matmul(dst, sl, mh, start=False, stop=stop)

            def x_halves(p, t):
                cols = slice(t * 128, (t + 1) * 128)
                return xt_h[p][:, cols], xt_l[p][:, cols]

            def transpose_x(n, p):
                pe.wait_ge(s_xn.sem, s_xn.at(n, NT))
                if s_k_t.due(n - 1, 1):
                    pe.wait_ge(s_k_t.sem, s_k_t.at(n - 1, 1))
                for t in range(NT):
                    last = t_.transpose(ps_a[:, t * 128:(t + 1) * 128], xn[p][:, t, :], ident[:])
                last.then_inc(s_xt.sem, 1)

            def project(n, p, t):
                if t == 0:
                    pe.wait_ge(s_xt_l.sem, s_xt_l.at(n, 1))
                else:
                    pe.wait_ge(s_logits0.sem, s_logits0.at(n, t))
                three_passes(ps_a[:, 0:PROJ], x_halves(p, t), (proj_h[:], proj_l[:])).then_inc(s_proj.sem, 1)

            def gram(n, p, t):
                if t == 0:
                    pe.wait_ge(s_logits0.sem, s_logits0.at(n, NT))
                else:
                    pe.wait_ge(s_var_raw.sem, s_var_raw.at(n, t * EXPERTS))
                three_passes(ps_a[:], x_halves(p, t), (gram_h[:], gram_l[:])).then_inc(s_gram.sem, 1)

            def transpose_std(n):
                pe.wait_ge(s_std_cols.sem, s_std_cols.at(n, 3))
                pe.wait_ge(s_var_raw.sem, s_var_raw.at(n, NV))
                for t in range(NT):
                    last = t_.transpose(ps_a[0:96, t * 128:(t + 1) * 128], std_cols[:, t, :], ident[:])
                last.then_inc(s_std_ps.sem, 1)

            def transpose_stack(n, which, done, free):
                pe.wait_ge(s_stack.sem, s_stack.at(n, 2))
                pe.wait_ge(free.sem, free.at(n, 1))
                dst = ps_a[:].bitcast(F16)
                for g in range(NG):
                    for t in range(NT):
                        rows = stack[:, t, which, g * NC:(g + 1) * NC].rearrange("p c s d -> p (c s d)")
                        at = g * SEQ + t * 128
                        last = t_.transpose(dst[:, at:at + 128], rows, ident16[:])
                last.then_inc(done.sem, 1)

            def scores(j, p, g):
                if g == 0:
                    pe.wait_ge(s_q_t.sem, s_q_t.at(j, 1))
                    pe.wait_ge(s_k_t.sem, s_k_t.at(j, 1))
                if s_probs.due(j, 2 * g):
                    pe.wait_ge(s_probs.sem, s_probs.at(j, 2 * g))
                for c in range(NC):
                    r = slice(32 * c, 32 * c + 32)
                    t_.matmul(ps_s[:, c, 128:384], k_t[p][r, g, 0:128], q_t[p][r, g, :], start=True, stop=True)
                for c in range(NC):
                    r = slice(32 * c, 32 * c + 32)
                    last = t_.matmul(ps_s[:, c, 0:128], k_t[p][r, g, 128:256], q_t[p][r, g, 128:256],
                                     start=True, stop=True)
                    if c % 2:
                        last.then_inc(s_scores.sem, 1)

            def weigh_values(j, p, g):
                pe.wait_ge(s_masked.sem, s_masked.at(j, 2 * g + 2))
                if g == 0:
                    if s_z_t.due(j - 1, 1):
                        pe.wait_ge(s_z_t.sem, s_z_t.at(j - 1, 1))
                for t in range(NT):
                    for c in range(NC):
                        at = (g * NC + c) * 32
                        q0 = 0 if t == 0 else 128
                        cols = slice(128, 384) if t == 0 else slice(0, 128)
                        last = t_.matmul(ps_z[32 * c:32 * c + 32, q0:SEQ], vz[p][:, t, at:at + 32],
                                         probs[g % 2][:, c, cols], start=(g == 0 and t == 0),
                                         stop=(g == NG - 1 and t == NT - 1), skip_group_check=True)
                last.then_inc(s_pv.sem, 1)

            def hidden(j, p, e):
                if e == 0:
                    pe.wait_ge(s_std_t.sem, s_std_t.at(j, 1))
                    if s_relu[1].due(j - 1, NG // 2):
                        pe.wait_ge(s_relu[1].sem, s_relu[1].at(j - 1, NG // 2))
                else:
                    pe.wait_ge(s_relu[(e - 1) % 2].sem, s_relu[(e - 1) % 2].at(j, (e - 1) // 2 + 1))
                for c in range(CH):
                    cols = slice((e * CH + c) * 128, (e * CH + c + 1) * 128)
                    dst = ps_h[:, c * SEQ:(c + 1) * SEQ]
                    three_passes(dst, (w1_h[:, cols], w1_l[:, cols]), (xt_h[p][:], xt_l[p][:]), stop=False)
                    last = t_.matmul(dst, b_rows[:, cols], std_t[p][:], start=False, stop=True)
                last.then_inc(s_hid.sem, 1)

            def expert_out(j, p, e):
                pe.wait_ge(s_relu[e % 2].sem, s_relu[e % 2].at(j, e // 2 + 1))
                if e == 0:
                    if s_base2.due(j - 1, 1):
                        pe.wait_ge(s_base2.sem, s_base2.at(j - 1, 1))
                else:
                    pe.wait_ge(s_acc.sem, s_acc.at(j, e * NT))
                for t in range(NT):
                    for c in range(CH):
                        at = c * SEQ + t * 128
                        last = t_.matmul(ps_o[:, t * D:(t + 1) * D], hid_t[e % 2][:, at:at + 128],
                                         w2_sb[:, e * CH + c, :], start=(c == 0), stop=(c == CH - 1))
                last.then_inc(s_expert.sem, 1)

            def attention_out(j):
                pe.wait_ge(s_z_t.sem, s_z_t.at(j, 1))
                for t in range(NT):
                    at = (NT + t) * D
                    last = t_.matmul(ps_o[:, at:at + D], z_t[:, t * 128:(t + 1) * 128], wo_t[:],
                                     start=True, stop=True)
                last.then_inc(s_attn.sem, 1)

            def batch(j, p):
                n, n2 = j + 1, j + 2
                for g in range(NG):
                    jj, pp, gg = (j, p, g + 1) if g < NG - 1 else (n, 1 - p, 0)
                    if exists(jj):
                        hidden(jj, pp, gg)
                    if exists(n):
                        if g == 0:
                            project(n, 1 - p, 0)
                        elif g == 1:
                            gram(n, 1 - p, 1)
                        elif g == 2:
                            transpose_std(n)
                    if exists(jj):
                        scores(jj, pp, gg)
                    if exists(n):
                        if g == 0:
                            project(n, 1 - p, 1)
                        elif g == 2:
                            transpose_stack(n, 0, s_q_ps, s_std_t)
                    if exists(j):
                        weigh_values(j, p, g)
                    if exists(n):
                        if g == 0:
                            gram(n, 1 - p, 0)
                        elif g == 2:
                            transpose_stack(n, 1, s_k_ps, s_q_t)
                    if g == 3 and exists(n2):
                        transpose_x(n2, p)
                    if exists(j):
                        expert_out(j, p, g)
                if exists(j):
                    attention_out(j)

            setup()
            batches(pe, batch, -2, 0)


def kernel(**inputs):
    import concourse.bacc as bacc
    from concourse.bass_utils import run_bass_kernel_spmd

    names = ["x", "Wq", "bq", "Wk", "bk", "Wv", "bv", "Wo", "norm_w"]
    names = [f"L0_attn_{n}" for n in names]
    names += [f"L0_ffn_{n}" for n in ("router_w", "rn_g", "rn_b", "w1", "ln_g", "ln_b", "w2", "on_g", "on_b")]
    inv_freq = (1.0 / np.float32(10000.0) ** (np.arange(0, DH, 2, dtype=np.float32) / np.float32(DH))).astype(np.float32)
    freqs = np.outer(np.arange(SEQ, dtype=np.float32), inv_freq).astype(np.float32)
    emb = np.concatenate([freqs, freqs], -1)
    sign = np.where(np.arange(DH) % 2 == 0, -1.0, 1.0).astype(np.float32)
    rope_c = np.stack([np.cos(emb), sign * np.sin(emb)]).astype(np.float32)
    rope_c = np.ascontiguousarray(rope_c.reshape(2, NT, 128, DH).transpose(2, 0, 1, 3))
    consts = {
        "identity": np.eye(128, dtype=np.float32),
        "rope": rope_c,
        "earlier": np.tril(np.ones((EXPERTS, EXPERTS), np.float32), -1),
    }
    nc = bacc.Bacc("TRN2", target_bir_lowering=False, num_devices=1)
    arrays, args = {}, []
    for name, a in [(n, np.ascontiguousarray(inputs[n])) for n in names] + list(consts.items()):
        arrays[f"in_{name}"] = a
        args.append(nc.dram_tensor(f"in_{name}", a.shape, mybir.dt.from_np(a.dtype), kind="ExternalInput").ap())
    out = nc.dram_tensor("out", (B, SEQ, D), F32, kind="ExternalOutput").ap()
    build(nc, *args, out)
    result = run_bass_kernel_spmd(nc, [arrays], core_ids=[0])
    return result.results[0]["out"]
```

```python
from contextlib import ExitStack

import numpy as np

import concourse.bass as bass
from concourse import mybir

F32 = mybir.dt.float32
F32R = mybir.dt.float32r
F16 = mybir.dt.float16
ALU = mybir.AluOpType
ACT = mybir.ActivationFunctionType
AX_X = mybir.AxisListType.X

B, SEQ, D = 32, 256, 128
NT = SEQ // 128
HEADS, DH = 16, 8
NG = 4
NC = HEADS // NG
EXPERTS, HID = 4, 256
CH = HID // 128
SLOTS = 4
QKV = 3 * D
PROJ = QKV + EXPERTS
EPS_LN = 1e-5
EPS_RMS = float(np.finfo(np.float32).eps)
EPS_GATE = 1e-8
QK_SCALE = 16.0


class Signal:

    def __init__(self, sem, per):
        self.sem, self.per = sem, per

    def at(self, j, n):
        return j * self.per + n

    def due(self, j, n):
        value = self.at(j, n)
        return not isinstance(value, int) or value > 0


def build(nc, x, wq, bq, wk, bk, wv, bv, wo, norm_w, router_w, rn_g, rn_b, w1, ln_g, ln_b, w2,
          on_g, on_b, ident_c, rope_c, earlier_c, out):
    ctx = ExitStack()
    with ctx:
        def sb(name, shape, dt=F32):
            return ctx.enter_context(nc.sbuf_tensor(name, shape, dt))

        def ps(name, shape):
            return ctx.enter_context(nc.psum_tensor(name, shape, F32))

        def signal(name, per):
            return Signal(ctx.enter_context(nc.semaphore(name)), per)

        ident = sb("ident", [128, 128])
        ident16 = sb("ident16", [128, 128], F16)
        rope = sb("rope", [128, 2, NT, DH])
        earlier = sb("earlier", [128, EXPERTS, EXPERTS])
        w_raw = sb("w_raw", [128, 4, D])
        bias_raw = sb("bias_raw", [128, 3, D])
        bias = sb("bias", [128, QKV])
        router_raw = sb("router_raw", [EXPERTS, D])
        rn_cols = sb("rn_cols", [128, 2])
        w1_raw = sb("w1_raw", [128, EXPERTS, HID])
        w1_c = sb("w1_c", [128, EXPERTS, HID])
        w1_g = sb("w1_g", [128, EXPERTS, HID])
        w1_mean = sb("w1_mean", [128, EXPERTS])
        w1_ct = sb("w1_ct", [128, EXPERTS * CH, D])
        ln_g_all = sb("ln_g_all", [128, EXPERTS, HID])
        b_raw = sb("b_raw", [128, EXPERTS * HID])
        w2_sb = sb("w2_sb", [128, EXPERTS * CH, D])
        on_gb = sb("on_gb", [128, 2, D])
        nw = sb("nw", [128, DH])
        nw_m = sb("nw_m", [128, 4])
        nw_s = sb("nw_s", [128, DH])
        proj_h = sb("proj_h", [128, PROJ], F32R)
        proj_l = sb("proj_l", [128, PROJ], F32R)
        router_t = sb("router_t", [128, EXPERTS])
        router_g = sb("router_g", [128, EXPERTS])
        rn_b_all = sb("rn_b_all", [128, 128])
        router_b = sb("router_b", [128, EXPERTS])
        wo_t = sb("wo_t", [128, D])
        w1_h = sb("w1_h", [128, EXPERTS * HID], F32R)
        w1_l = sb("w1_l", [128, EXPERTS * HID], F32R)
        gram_h = sb("gram_h", [128, EXPERTS * D], F32R)
        gram_l = sb("gram_l", [128, EXPERTS * D], F32R)
        b_rows = sb("b_rows", [128, EXPERTS * HID], F32R)
        cos_t = sb("cos_t", [128, NT, DH])
        sin_t = sb("sin_t", [128, NT, DH])

        x_in = [sb(f"x_in{p}", [128, NT, D]) for p in range(2)]
        xn = [sb(f"xn{p}", [128, NT, D]) for p in range(2)]
        x_hi = sb("x_hi", [128, NT, D], F32R)
        x_low2 = [sb(f"x_low2{p}", [128, NT, D]) for p in range(2)]
        xt_h = [sb(f"xt_h{p}", [128, SEQ], F32R) for p in range(2)]
        xt_l = [sb(f"xt_l{p}", [128, SEQ], F32R) for p in range(2)]
        vz = [sb(f"vz{p}", [128, NT, NG * 136]) for p in range(2)]
        qk_t = [sb(f"qk_t{p}", [128, 2 * NG, SEQ], F16) for p in range(2)]
        std_t = [sb(f"std_t{p}", [128, SEQ], F32R) for p in range(2)]
        scale_e = [sb(f"scale_e{p}", [128, NT, EXPERTS]) for p in range(2)]
        stats = sb("stats", [128, 2 * NT, 6])
        mean_var = sb("mean_var", [128, 2 * NT, 2])
        NM = NT * 2 * HEADS
        root1_in = sb("root1_in", [128, NM + 2 * NT])
        root1_ln = sb("root1_ln", [128, NM + 2 * NT])
        root1_r = sb("root1_r", [128, NM + 2 * NT])
        root1_a = sb("root1_a", [128, NM + 2 * NT])
        root1_b = sb("root1_b", [128, NM + 2 * NT])
        root1 = sb("root1", [128, NM + 2 * NT])
        rms, rstd_f, rstd_x = root1[:, 0:NM], root1[:, NM:NM + NT], root1[:, NM + NT:NM + 2 * NT]
        qk = sb("qk", [128, NT, 2 * D])
        logits0 = sb("logits0", [128, NT, EXPERTS])
        qk_sq = sb("qk_sq", [128, NT, 2 * D])
        ms_sum = sb("ms_sum", [128, NM])
        rope_qk = sb("rope_qk", [128, NT * 2 * D])
        rope1 = sb("rope1", [128, NT * 2 * D])
        rope2 = sb("rope2", [128, NT * 2 * D])
        qk_r = sb("qk_r", [128, NT * 2 * D])
        stack = sb("stack", [128, NT, 2, HEADS, SLOTS, DH], F16)
        NV = NT * EXPERTS
        scrap = sb("scrap", [128, NV, D])
        var = [sb(f"var{p}", [128, NV + NT]) for p in range(2)]
        rt1 = sb("rt1", [128, NT])
        root2_in = sb("root2_in", [128, NV + NT])
        root2_ln = sb("root2_ln", [128, NV + NT])
        root2_r = sb("root2_r", [128, NV + NT])
        root2_a = sb("root2_a", [128, NV + NT])
        root2_b = sb("root2_b", [128, NV + NT])
        root2 = sb("root2", [128, NV + NT])
        std = sb("std", [128, NV])
        std_cols = sb("std_cols", [128, NT, 96])
        lg2 = sb("lg2", [128, NT, EXPERTS])
        lg_max = sb("lg_max", [128, NT])
        lg3 = sb("lg3", [128, NT, EXPERTS])
        gate = sb("gate", [128, NT, EXPERTS])
        gate_sum = sb("gate_sum", [128, NT])
        ahead = sb("ahead", [128, NT, EXPERTS, EXPERTS])
        tied = sb("tied", [128, NT, EXPERTS, EXPERTS])
        beaten = sb("beaten", [128, NT, EXPERTS, EXPERTS])
        rank = sb("rank", [128, NV])
        chosen = sb("chosen", [128, NT, EXPERTS])
        chosen_sum = sb("chosen_sum", [128, NT])
        gate_den = sb("gate_den", [128, NT])
        gate_inv = sb("gate_inv", [128, NT])
        probs = [sb(f"probs{b}", [128, NC, 3 * 128]) for b in range(2)]
        hid_t = [sb(f"hid_t{b}", [128, CH * SEQ]) for b in range(2)]
        acc = [sb(f"acc{p}", [128, NT, D]) for p in range(2)]
        z_t = sb("z_t", [128, SEQ])
        ffn_n = sb("ffn_n", [128, NT, D])
        ffn_g = sb("ffn_g", [128, NT, D])
        base0 = sb("base0", [128, NT, D])
        base1 = [sb(f"base1_{p}", [128, NT, D]) for p in range(2)]
        base2 = sb("base2", [128, NT, D])
        y = [sb(f"y{p}", [128, NT, D]) for p in range(2)]

        ps_s = ps("ps_s", [128, NC, 512])
        ps_z = ps("ps_z", [128, 512])
        ps_h = ps("ps_h", [128, 512])
        ps_o = ps("ps_o", [128, 512])
        ps_a = ps("ps_a", [128, 512])

        LOADS = 19
        loaded = signal("loaded", 16 * LOADS)
        b_loaded = signal("b_loaded", 16 * 3 * EXPERTS)
        v_chain = signal("v_chain", 1)
        zeroed = signal("zeroed", 1)
        v_setup = signal("v_setup", 1)
        p_setup = signal("p_setup", 1)
        x_loaded = [signal(f"x_loaded{p}", 16 // 2) for p in range(2)]
        y_stored = [signal(f"y_stored{p}", 16 // 2) for p in range(2)]
        s_stats_x = signal("s_stats_x", NT)
        s_stats_f = signal("s_stats_f", NT)
        s_mean_var_x = signal("s_mean_var_x", NT)
        s_mean_var_f = signal("s_mean_var_f", NT)
        s_root1_in = signal("s_root1_in", 1)
        s_root1_ln = signal("s_root1_ln", 1)
        s_root1_r = signal("s_root1_r", 1)
        s_root1 = signal("s_root1", 3)
        s_xn = signal("s_xn", NT)
        s_xt = signal("s_xt", 1)
        s_xt_h = signal("s_xt_h", 1)
        s_xt_l = signal("s_xt_l", 1)
        s_proj = signal("s_proj", NT)
        s_qk = signal("s_qk", NT)
        s_v = signal("s_v", NT)
        s_logits0 = signal("s_logits0", NT)
        s_qk_sq = signal("s_qk_sq", 1)
        s_ms = signal("s_ms", 2)
        s_rope_qk = signal("s_rope_qk", 1)
        s_rope1 = signal("s_rope1", 1)
        s_rope2 = signal("s_rope2", 1)
        s_qk_r = signal("s_qk_r", 1)
        s_high = signal("s_high", 1)
        s_low = signal("s_low", 1)
        s_stack = signal("s_stack", 2)
        s_stack_ps = signal("s_stack_ps", 2)
        s_qk_t = signal("s_qk_t", 2)
        s_gram = signal("s_gram", NT)
        s_var = signal("s_var", NV)
        s_router_var = signal("s_router_var", 2)
        s_root2_in = signal("s_root2_in", 1)
        s_root2_ln = signal("s_root2_ln", 1)
        s_root2_r = signal("s_root2_r", 1)
        s_root2 = signal("s_root2", 3)
        s_std = signal("s_std", 1)
        s_std_cols = signal("s_std_cols", 3)
        s_std_ps = signal("s_std_ps", 1)
        s_std_t = signal("s_std_t", 1)
        s_lg = signal("s_lg", 4)
        s_gate = signal("s_gate", 1)
        s_gate_sum = signal("s_gate_sum", 1)
        s_rank = signal("s_rank", 4)
        s_weight = signal("s_weight", 4)
        s_scale_e = signal("s_scale_e", NT)
        s_scores = signal("s_scores", 2 * NG)
        s_probs = signal("s_probs", 2 * NG)
        s_masked = signal("s_masked", 2 * NG)
        s_pv = signal("s_pv", NG)
        s_hid = signal("s_hid", NG)
        s_relu = signal("s_relu", NG)
        s_expert = signal("s_expert", NG)
        s_acc = signal("s_acc", NG * NT)
        s_z_t = signal("s_z_t", 1)
        s_attn = signal("s_attn", 1)
        s_base0 = signal("s_base0", 1)
        s_base1 = signal("s_base1", 1)
        s_base2 = signal("s_base2", 1)
        s_ffn_n = signal("s_ffn_n", NT)
        s_ffn_g = signal("s_ffn_g", 1)
        s_y = signal("s_y", 1)

        s_x_high = signal("s_x_high", 1)
        s_x_low2 = signal("s_x_low2", 1)

        x_v = x.rearrange("b (t p) d -> p (b t) d", p=128)
        out_v = out.rearrange("b (t p) d -> p (b t) d", p=128)
        V_CENTRED, V_ROUTER_T, V_W1_CT, V_DONE = 1, 2, 3, 4
        P_WEIGHTS, P_W1_CT, P_GRAM, P_ROUTER_B = 1, 2, 3, 4

        block = ctx.enter_context(nc.Block())

        def batches(eng, batch, first, straight_after, tail=2):
            for j in range(first, 4):
                batch(j, j % 2)
            with eng.Fori(2, (B - tail) // 2) as i:
                for p in range(2):
                    batch(i * 2 + p, p)
            for j in range(B - tail, B + straight_after):
                batch(j, j % 2)

        def known(j):
            return isinstance(j, int)

        def exists(j):
            return not known(j) or 0 <= j < B

        @block.sync
        def _(sp):
            for p in range(2):
                sp.dma_start(x_in[p][:], x_v[:, p * NT:(p + 1) * NT, :]).then_inc(x_loaded[p].sem, 16)

            def load(dst, src):
                sp.dma_start(dst, src).then_inc(loaded.sem, 16)

            load(ident[:], ident_c)
            for n, w in enumerate((wq, wk, wv, wo)):
                load(w_raw[:, n, :], w)
            load(w1_raw[:], w1.rearrange("e d h -> d e h"))
            load(nw[:], norm_w.partition_broadcast(128))
            load(router_raw[:], router_w)
            load(rn_cols[:, 0:1], rn_g.unsqueeze(1))
            load(rn_cols[:, 1:2], rn_b.unsqueeze(1))
            load(rope[:], rope_c)
            load(earlier[:], earlier_c.partition_broadcast(128))
            for n, b in enumerate((bq, bk, bv)):
                load(bias_raw[:, n, :], b.partition_broadcast(128))
            load(ln_g_all[:], ln_g.partition_broadcast(128))
            load(w2_sb[:], w2.rearrange("e (c h) d -> h (e c) d", h=128))
            load(on_gb[:, 0, :], on_g.partition_broadcast(128))
            load(on_gb[:, 1, :], on_b.partition_broadcast(128))
            sp.wait_ge(zeroed.sem, 1)
            for quadrant in range(3):
                for e in range(EXPERTS):
                    r = 32 * quadrant + e
                    sp.dma_start(b_raw[r:r + 1, e * HID:(e + 1) * HID],
                                 ln_b[e:e + 1, :]).then_inc(b_loaded.sem, 16)

            def batch(j, p):
                n, q = j + 1, 1 - p
                if exists(n) and exists(n + 2):
                    if s_base0.due(n, 1):
                        sp.wait_ge(s_base0.sem, s_base0.at(n, 1))
                    sp.dma_start(x_in[q][:], x_v[:, bass.ds((n + 2) * NT, NT), :]).then_inc(x_loaded[q].sem, 16)
                if exists(j - 1):
                    sp.wait_ge(s_y.sem, s_y.at(j - 1, 1))
                    sp.dma_start(out_v[:, bass.ds((j - 1) * NT, NT), :], y[q][:]).then_inc(y_stored[q].sem, 16)

            batches(sp, batch, -2, 1, tail=4)
            for p in range(2):
                sp.wait_ge(y_stored[p].sem, y_stored[p].at(B - 2, 16))

        @block.vector
        def _(dve):
            v = nc.vector
            chain = [0]

            def link(ins):
                chain[0] += 1
                ins.then_inc(v_chain.sem, 1)
                dve.wait_ge(v_chain.sem, chain[0])

            def perm(ap):
                return ap.rearrange("p (c g d) -> p g c d", c=NC, g=NG)

            def rows(ap):
                return ap.rearrange("p (g c d) -> p g c d", c=NC, g=NG)

            def setup():
                v.memset(b_raw[:], 0.0).then_inc(zeroed.sem, 1)
                for p in range(2):
                    link(v.memset(vz[p][:], 0.0))
                    link(v.memset(std_t[p][:].bitcast(F32), 0.0))
                link(v.memset(std_cols[:], 0.0))
                link(v.memset(mean_var[:], 0.0))
                link(v.memset(root1_in[:], 1.0))
                dve.wait_ge(loaded.sem, 16 * LOADS)
                link(v.tensor_reduce(w1_mean[:], w1_raw[:], AX_X, ALU.add))
                link(v.tensor_scalar(w1_mean[:], w1_mean[:], 1.0 / HID, None, ALU.mult))
                v.tensor_tensor(w1_c[:], w1_raw[:], w1_mean[:].unsqueeze(2).to_broadcast([128, EXPERTS, HID]),
                                ALU.subtract).then_inc(v_setup.sem, 1)
                dve.wait_ge(v_setup.sem, V_CENTRED)
                link(v.tensor_copy(ident16[:], ident[:]))
                link(v.tensor_reduce(nw_m[:, 0:1], nw[:], AX_X, ALU.max, apply_absolute_value=True))
                link(v.tensor_scalar(nw_m[:, 0:1], nw_m[:, 0:1], 1e-30, None, ALU.max))
                link(v.reciprocal(nw_m[:, 1:2], nw_m[:, 0:1]))
                link(v.tensor_tensor(nw_m[:, 2:3], nw_m[:, 0:1], nw_m[:, 0:1], ALU.mult))
                link(v.tensor_tensor(nw_m[:, 3:4], nw_m[:, 2:3], nw_m[:, 2:3], ALU.mult))
                link(v.tensor_scalar(nw_s[:], nw[:], nw_m[:, 1:2], QK_SCALE, ALU.mult, ALU.mult))
                link(v.tensor_tensor(cos_t[:], rope[:, 0], nw_s[:].unsqueeze(1).to_broadcast([128, NT, DH]),
                                     ALU.mult))
                nw_pairs = nw_s[:].rearrange("p (a two) -> p a two", two=2)
                for t in range(NT):
                    link(v.tensor_tensor(sin_t[:, t].rearrange("p (a two) -> p a two", two=2),
                                         rope[:, 1, t].rearrange("p (a two) -> p a two", two=2),
                                         nw_pairs[:, :, ::-1], ALU.mult))
                link(v.tensor_tensor(w1_g[:], w1_c[:], ln_g_all[:], ALU.mult))
                link(v.tensor_copy(w1_h[:], w1_g[:].rearrange("p e h -> p (e h)")))
                link(v.tensor_tensor(w1_l[:], w1_g[:].rearrange("p e h -> p (e h)"),
                                     w1_h[:].bitcast(F32), ALU.subtract))
                for n in range(2):
                    link(v.tensor_copy(rows(bias[:, n * D:(n + 1) * D]), perm(bias_raw[:, n, :])))
                link(v.tensor_copy(bias[:, 2 * D:QKV], bias_raw[:, 2, :]))
                link(v.tensor_copy(rn_b_all[:], rn_cols[:, 1:2].to_broadcast([128, 128])))
                dve.wait_ge(b_loaded.sem, 16 * 3 * EXPERTS)
                link(v.tensor_copy(b_rows[:], b_raw[:]))
                link(v.tensor_tensor(b_rows[64:96, :], b_raw[64:96, :],
                                     b_rows[64:96, :].bitcast(F32), ALU.subtract))
                dve.wait_ge(p_setup.sem, P_WEIGHTS)
                for n in range(2):
                    w_t = ps_s[:, 0, n * D:(n + 1) * D]
                    link(v.tensor_copy(rows(proj_h[:, n * D:(n + 1) * D]), perm(w_t)))
                    link(v.tensor_tensor(rows(proj_l[:, n * D:(n + 1) * D]), perm(w_t),
                                         rows(proj_h[:, n * D:(n + 1) * D]).bitcast(F32), ALU.subtract))
                w_t = ps_s[:, 0, 2 * D:3 * D]
                link(v.tensor_copy(proj_h[:, 2 * D:QKV], w_t))
                link(v.tensor_tensor(proj_l[:, 2 * D:QKV], w_t, proj_h[:, 2 * D:QKV].bitcast(F32), ALU.subtract))
                link(v.tensor_scalar(wo_t[:], ps_s[:, 0, 3 * D:4 * D], nw_m[:, 3:4], None, ALU.mult))
                v.tensor_copy(router_t[:], ps_s[:, 1, 0:EXPERTS]).then_inc(v_setup.sem, 1)
                dve.wait_ge(v_setup.sem, V_ROUTER_T)
                link(v.tensor_scalar(router_g[:], router_t[:], rn_cols[:, 0:1], None, ALU.mult))
                link(v.tensor_copy(proj_h[:, QKV:PROJ], router_g[:]))
                link(v.tensor_tensor(proj_l[:, QKV:PROJ], router_g[:], proj_h[:, QKV:PROJ].bitcast(F32),
                                     ALU.subtract))
                dve.wait_ge(p_setup.sem, P_W1_CT)
                v.tensor_copy(w1_ct[:].rearrange("p c d -> p (c d)"),
                              ps_s[:, 2:4, :].rearrange("p b n -> p (b n)")).then_inc(v_setup.sem, 1)
                dve.wait_ge(p_setup.sem, P_GRAM)
                link(v.tensor_scalar(gram_h[:], ps_h[:], 1.0 / HID, None, ALU.mult))
                link(v.scalar_tensor_tensor(gram_l[:], ps_h[:], 1.0 / HID, gram_h[:].bitcast(F32),
                                            ALU.mult, ALU.subtract))
                dve.wait_ge(p_setup.sem, P_ROUTER_B)
                v.tensor_copy(router_b[:], ps_o[:, 0:EXPERTS]).then_inc(v_setup.sem, 1)

            def newton(k, s, value, guess, a, b, result):
                if k == 0:
                    v.scalar_tensor_tensor(a, guess, -0.5, guess, ALU.mult, ALU.mult).then_inc(s.sem, 1)
                elif k == 1:
                    v.tensor_tensor(b, value, a, ALU.mult).then_inc(s.sem, 1)
                else:
                    v.scalar_tensor_tensor(result, b, 1.5, guess, ALU.add, ALU.mult).then_inc(s.sem, 1)

            def newton1(m, k):
                if k == 0:
                    dve.wait_ge(s_root1_r.sem, s_root1_r.at(m, 1))
                else:
                    dve.wait_ge(s_root1.sem, s_root1.at(m, k))
                newton(k, s_root1, root1_in[:], root1_r[:], root1_a[:], root1_b[:], root1[:])

            def newton2(n, k):
                if k == 0:
                    dve.wait_ge(s_root2_r.sem, s_root2_r.at(n, 1))
                else:
                    dve.wait_ge(s_root2.sem, s_root2.at(n, k))
                newton(k, s_root2, root2_in[:], root2_r[:], root2_a[:], root2_b[:], root2[:])

            def input_stats(n, p):
                dve.wait_ge(x_loaded[p].sem, x_loaded[p].at(n - p, 16))
                for t in range(NT):
                    v.bn_stats(stats[:, NT + t, :], x_in[p][:, t, :]).then_inc(s_stats_x.sem, 1)

            def input_moments(n):
                for t in range(NT):
                    dve.wait_ge(s_stats_x.sem, s_stats_x.at(n, t + 1))
                    dve.nop(nofuse=True)
                    v.bn_aggr(mean_var[:, NT + t, :], stats[:, NT + t, :]).then_inc(s_mean_var_x.sem, 1)

            def root1_input(m, has_x, has_f):
                if has_x:
                    dve.wait_ge(s_mean_var_x.sem, s_mean_var_x.at(m, NT))
                if has_f:
                    dve.wait_ge(s_mean_var_f.sem, s_mean_var_f.at(m - 3, NT))
                v.tensor_scalar(root1_in[:, NM:], mean_var[:, :, 1], EPS_LN, None, ALU.add).then_inc(s_root1_in.sem, 1)

            def input_norm(n, p):
                dve.wait_ge(s_root1.sem, s_root1.at(n, 3))
                if s_base0.due(n - 2, 1):
                    dve.wait_ge(s_base0.sem, s_base0.at(n - 2, 1))
                for t in range(NT):
                    v.tensor_scalar(xn[p][:, t, :], x_in[p][:, t, :], mean_var[:, NT + t, 0:1], rstd_x[:, t:t + 1],
                                    ALU.subtract, ALU.mult).then_inc(s_xn.sem, 1)

            def router_var(n, p, k):
                if k == 0:
                    dve.wait_ge(s_root1.sem, s_root1.at(n, 3))
                    v.tensor_tensor(rt1[:], mean_var[:, NT:, 1], rstd_x, ALU.mult).then_inc(s_router_var.sem, 1)
                else:
                    dve.wait_ge(s_router_var.sem, s_router_var.at(n, 1))
                    v.tensor_tensor(var[p][:, NV:], rt1[:], rstd_x, ALU.mult).then_inc(s_router_var.sem, 1)

            def xt_low(n, p):
                dve.wait_ge(s_xt_h.sem, s_xt_h.at(n, 1))
                if s_hid.due(n - 2, NG):
                    dve.wait_ge(s_hid.sem, s_hid.at(n - 2, NG))
                v.tensor_tensor(xt_l[p][:], ps_a[:, 0:SEQ], xt_h[p][:].bitcast(F32),
                                ALU.subtract).then_inc(s_xt_l.sem, 1)

            def take_projections(n, p, t):
                dve.wait_ge(s_proj.sem, s_proj.at(n, t + 1))
                v.tensor_tensor(qk[:, t, :], ps_a[:, 0:2 * D], bias[:, 0:2 * D], ALU.add).then_inc(s_qk.sem, 1)
                if s_pv.due(n - 2, NG):
                    dve.wait_ge(s_pv.sem, s_pv.at(n - 2, NG))
                v_blocks = vz[p][:, t, :].rearrange("p (g s) -> p g s", g=NG)[:, :, 0:NC * 32]
                v_blocks = v_blocks.rearrange("p g (c s) -> p g c s", c=NC)[:, :, :, 0:DH]
                v.tensor_tensor(v_blocks, perm(ps_a[:, 2 * D:QKV]), perm(bias[:, 2 * D:QKV]),
                                ALU.add).then_inc(s_v.sem, 1)
                v.tensor_copy(logits0[:, t, :], ps_a[:, QKV:PROJ]).then_inc(s_logits0.sem, 1)

            def rope_cos(n):
                dve.wait_ge(s_qk.sem, s_qk.at(n, NT))
                v.tensor_tensor(rope1[:].rearrange("p (t h d) -> p t h d", t=NT, d=DH),
                                qk[:].rearrange("p t (h d) -> p t h d", d=DH),
                                cos_t[:].unsqueeze(2).to_broadcast([128, NT, 2 * HEADS, DH]),
                                ALU.mult).then_inc(s_rope1.sem, 1)

            def mean_squares(n, k):
                if k == 0:
                    dve.wait_ge(s_qk_sq.sem, s_qk_sq.at(n, 1))
                    v.tensor_reduce(ms_sum[:], qk_sq[:].rearrange("p t (h d) -> p (t h) d", d=DH), AX_X,
                                    ALU.add).then_inc(s_ms.sem, 1)
                else:
                    dve.wait_ge(s_ms.sem, s_ms.at(n, 1))
                    v.tensor_scalar(root1_in[:, 0:NM], ms_sum[:], 1.0 / DH, EPS_RMS, ALU.mult,
                                    ALU.add).then_inc(s_ms.sem, 1)

            def rope_sum(n):
                dve.wait_ge(s_rope1.sem, s_rope1.at(n, 1))
                dve.wait_ge(s_rope2.sem, s_rope2.at(n, 1))
                v.tensor_tensor(rope_qk[:], rope1[:], rope2[:], ALU.add).then_inc(s_rope_qk.sem, 1)

            def rms_norm(n):
                dve.wait_ge(s_root1.sem, s_root1.at(n + 1, 3))
                dve.wait_ge(s_rope_qk.sem, s_rope_qk.at(n, 1))
                v.tensor_tensor(qk_r[:].rearrange("p (h d) -> p h d", d=DH),
                                rope_qk[:].rearrange("p (h d) -> p h d", d=DH),
                                rms.unsqueeze(2).to_broadcast([128, NM, DH]), ALU.mult).then_inc(s_qk_r.sem, 1)

            def stack_low(n):
                dve.wait_ge(s_high.sem, s_high.at(n, 1))
                high_low = stack[:].rearrange("p t k h s d -> p (t k h) s d")
                v.tensor_tensor(high_low[:, :, 1, :], qk_r[:].rearrange("p (h d) -> p h d", d=DH),
                                high_low[:, :, 0, :], ALU.subtract).then_inc(s_low.sem, 1)

            def stack_k(n):
                dve.wait_ge(s_low.sem, s_low.at(n, 1))
                k_rows = stack[:, :, 1]
                v.tensor_copy(k_rows[:, :, :, 2:4, :].rearrange("p t h s d -> p t h (s d)"),
                              k_rows[:, :, :, 0:2, :].rearrange("p t h s d -> p t h (s d)")).then_inc(s_stack.sem, 1)

            def stack_q(n):
                q_rows = stack[:, :, 0]
                for t in range(NT):
                    last = v.tensor_copy(q_rows[:, t, :, 2:4, :], q_rows[:, t, :, 1::-1, :])
                last.then_inc(s_stack.sem, 1)

            def x_twice_low(n, p):
                dve.wait_ge(s_x_high.sem, s_x_high.at(n, 1))
                v.scalar_tensor_tensor(x_low2[p][:], xn[p][:], 2.0, x_hi[:].bitcast(F32), ALU.mult,
                                        ALU.subtract).then_inc(s_x_low2.sem, 1)

            def variances(n, p, t):
                dve.wait_ge(s_gram.sem, s_gram.at(n, t + 1))
                if t == 0:
                    dve.wait_ge(s_x_low2.sem, s_x_low2.at(n, 1))
                for e in range(EXPERTS):
                    k = t * EXPERTS + e
                    v.tensor_tensor_reduce(out=scrap[:, k, :], in0=ps_a[:, e * D:(e + 1) * D],
                                           in1=x_low2[p][:, t, :], scale=1.0, scalar=0.0, op0=ALU.mult,
                                           op1=ALU.add, accum_out=var[p][:, k:k + 1]).then_inc(s_var.sem, 1)

            def root2_input(n, p):
                dve.wait_ge(s_var.sem, s_var.at(n, NV))
                dve.wait_ge(s_router_var.sem, s_router_var.at(n, 2))
                v.tensor_scalar(root2_in[:], var[p][:], EPS_LN, None, ALU.add).then_inc(s_root2_in.sem, 1)

            std3 = std[:].rearrange("p (t e) -> p t e", t=NT)
            std_high = std_cols[:, :, 0:EXPERTS]

            def hidden_std(n):
                dve.wait_ge(s_root2.sem, s_root2.at(n, 3))
                v.tensor_tensor(std[:], root2_in[:, 0:NV], root2[:, 0:NV], ALU.mult).then_inc(s_std.sem, 1)

            def std_columns(n, k):
                if k == 0:
                    dve.wait_ge(s_std.sem, s_std.at(n, 1))
                    if s_std_ps.due(n - 1, 1):
                        dve.wait_ge(s_std_ps.sem, s_std_ps.at(n - 1, 1))
                    v.tensor_copy(std_high.bitcast(F32R), std3).then_inc(s_std_cols.sem, 1)
                else:
                    dve.wait_ge(s_std_cols.sem, s_std_cols.at(n, 1))
                    v.tensor_tensor(std_cols[:, :, 32:32 + EXPERTS], std3, std_high,
                                    ALU.subtract).then_inc(s_std_cols.sem, 1)
                    v.tensor_copy(std_cols[:, :, 64:64 + EXPERTS], std_high).then_inc(s_std_cols.sem, 1)

            both, square = [128, NT, EXPERTS], [128, NT, EXPERTS, EXPERTS]

            def router_logits(n, k):
                if k == 0:
                    dve.wait_ge(s_root2.sem, s_root2.at(n, 3))
                    for t in range(NT):
                        v.scalar_tensor_tensor(lg2[:, t, :], logits0[:, t, :], root2[:, NV + t:NV + t + 1], router_b[:],
                                               ALU.mult, ALU.add).then_inc(s_lg.sem, 1)
                elif k == 1:
                    dve.wait_ge(s_lg.sem, s_lg.at(n, NT))
                    v.tensor_reduce(lg_max[:], lg2[:], AX_X, ALU.max).then_inc(s_lg.sem, 1)
                else:
                    dve.wait_ge(s_lg.sem, s_lg.at(n, NT + 1))
                    v.tensor_tensor(lg3[:], lg2[:], lg_max[:].unsqueeze(2).to_broadcast(both),
                                    ALU.subtract).then_inc(s_lg.sem, 1)

            def router_rank(n, k):
                if k == 0:
                    dve.wait_ge(s_lg.sem, s_lg.at(n, NT))
                    v.tensor_tensor(ahead[:], lg2[:].unsqueeze(2).to_broadcast(square),
                                    lg2[:].unsqueeze(3).to_broadcast(square), ALU.subtract).then_inc(s_rank.sem, 1)
                    return
                dve.wait_ge(s_rank.sem, s_rank.at(n, k))
                flat = "p t i j -> p (t i j)"
                if k == 1:
                    v.scalar_tensor_tensor(tied[:].rearrange(flat), ahead[:].rearrange(flat), 0.0,
                                           earlier[:].rearrange("p i j -> p (i j)").unsqueeze(1)
                                           .to_broadcast([128, NT, EXPERTS * EXPERTS]),
                                           ALU.is_equal, ALU.mult).then_inc(s_rank.sem, 1)
                elif k == 2:
                    v.scalar_tensor_tensor(beaten[:].rearrange(flat), ahead[:].rearrange(flat), 0.0,
                                           tied[:].rearrange(flat), ALU.is_gt, ALU.add).then_inc(s_rank.sem, 1)
                else:
                    v.tensor_reduce(rank[:], beaten[:].rearrange("p t i j -> p (t i) j"), AX_X,
                                    ALU.add).then_inc(s_rank.sem, 1)

            def gate_total(n):
                dve.wait_ge(s_gate.sem, s_gate.at(n, 1))
                v.tensor_reduce(gate_sum[:], gate[:], AX_X, ALU.add).then_inc(s_gate_sum.sem, 1)

            def router_weights(n, p, k):
                if k == 0:
                    dve.wait_ge(s_rank.sem, s_rank.at(n, 4))
                    v.scalar_tensor_tensor(chosen[:].rearrange("p t e -> p (t e)"), rank[:], 2.0,
                                           gate[:].rearrange("p t e -> p (t e)"), ALU.is_lt,
                                           ALU.mult).then_inc(s_weight.sem, 1)
                    return
                dve.wait_ge(s_weight.sem, s_weight.at(n, k))
                if k == 1:
                    v.tensor_reduce(chosen_sum[:], chosen[:], AX_X, ALU.add).then_inc(s_weight.sem, 1)
                elif k == 2:
                    dve.wait_ge(s_gate_sum.sem, s_gate_sum.at(n, 1))
                    v.scalar_tensor_tensor(gate_den[:], gate_sum[:], EPS_GATE, chosen_sum[:], ALU.mult,
                                           ALU.add).then_inc(s_weight.sem, 1)
                elif k == 3:
                    v.reciprocal(gate_inv[:], gate_den[:]).then_inc(s_weight.sem, 1)
                else:
                    for t in range(NT):
                        v.scalar_tensor_tensor(scale_e[p][:, t, :], chosen[:, t, :], gate_inv[:, t:t + 1],
                                               root2[:, t * EXPERTS:(t + 1) * EXPERTS], ALU.mult,
                                               ALU.mult).then_inc(s_scale_e.sem, 1)

            def combine(j, p, e, t):
                o = ps_o[:, t * D:(t + 1) * D]
                s = scale_e[p][:, t, e:e + 1]
                if e == 0:
                    if t == 0:
                        dve.wait_ge(s_expert.sem, s_expert.at(j, 1))
                        dve.wait_ge(s_scale_e.sem, s_scale_e.at(j, NT))
                        if s_ffn_n.due(j - 2, NT):
                            dve.wait_ge(s_ffn_n.sem, s_ffn_n.at(j - 2, NT))
                    v.tensor_scalar(acc[p][:, t, :], o, s, None, ALU.mult).then_inc(s_acc.sem, 1)
                    return
                if t == 0:
                    dve.wait_ge(s_expert.sem, s_expert.at(j, e + 1))
                if t == 0 and e == EXPERTS - 1:
                    dve.wait_ge(s_attn.sem, s_attn.at(j, 1))
                dve.wait_ge(s_acc.sem, s_acc.at(j, e * NT - NT + t + 1))
                v.scalar_tensor_tensor(acc[p][:, t, :], o, s, acc[p][:, t, :], ALU.mult, ALU.add).then_inc(s_acc.sem, 1)

            def add_attention(j, p):
                dve.wait_ge(s_base1.sem, s_base1.at(j, 1))
                if s_y.due(j - 1, 1):
                    dve.wait_ge(s_y.sem, s_y.at(j - 1, 1))
                v.tensor_tensor(base2[:].rearrange("p t d -> p (t d)"), ps_o[:, NT * D:2 * NT * D],
                                base1[p][:].rearrange("p t d -> p (t d)"), ALU.add).then_inc(s_base2.sem, 1)

            def output_stats(j, p):
                for t in range(NT):
                    dve.wait_ge(s_acc.sem, s_acc.at(j, (EXPERTS - 1) * NT + t + 1))
                    v.bn_stats(stats[:, t, :], acc[p][:, t, :]).then_inc(s_stats_f.sem, 1)

            def output_moments(j):
                for t in range(NT):
                    dve.wait_ge(s_stats_f.sem, s_stats_f.at(j, t + 1))
                    dve.nop(nofuse=True)
                    v.bn_aggr(mean_var[:, t, :], stats[:, t, :]).then_inc(s_mean_var_f.sem, 1)

            def output_norm(j, p):
                dve.wait_ge(s_root1.sem, s_root1.at(j + 3, 3))
                if s_ffn_g.due(j - 1, 1):
                    dve.wait_ge(s_ffn_g.sem, s_ffn_g.at(j - 1, 1))
                for t in range(NT):
                    v.tensor_scalar(ffn_n[:, t, :], acc[p][:, t, :], mean_var[:, t, 0:1], rstd_f[:, t:t + 1],
                                    ALU.subtract, ALU.mult).then_inc(s_ffn_n.sem, 1)

            def batch(j, p):
                h, n, m, q = j - 1, j + 1, j + 2, 1 - p
                has_h, has_j, has_n, has_m = exists(h), exists(j), exists(n), exists(m)
                if has_j:
                    newton2(j, 2)
                    hidden_std(j)
                if has_h:
                    combine(h, q, 1, 0)
                    combine(h, q, 1, 1)
                if has_j:
                    router_logits(j, 0)
                    std_columns(j, 0)
                    router_rank(j, 0)
                    std_columns(j, 1)
                    router_rank(j, 1)
                    router_logits(j, 1)
                    router_logits(j, 2)
                if has_h:
                    combine(h, q, 2, 0)
                if has_n:
                    router_var(n, q, 0)
                if has_h:
                    combine(h, q, 2, 1)
                if has_j:
                    router_rank(j, 2)
                    gate_total(j)
                    router_rank(j, 3)
                    router_weights(j, p, 0)
                if has_n:
                    x_twice_low(n, q)
                    xt_low(n, q)
                if has_m:
                    input_stats(m, p)
                if has_h:
                    combine(h, q, 3, 0)
                    combine(h, q, 3, 1)
                if has_n:
                    take_projections(n, q, 0)
                if has_h:
                    output_stats(h, q)
                    add_attention(h, q)
                if has_m:
                    input_moments(m)
                if has_n:
                    take_projections(n, q, 1)
                if has_h:
                    output_moments(h)
                if has_j:
                    router_weights(j, p, 1)
                if has_n:
                    router_var(n, q, 1)
                    rope_cos(n)
                root1_input(m, exists(m), exists(m - 3))
                if has_n:
                    mean_squares(n, 0)
                    mean_squares(n, 1)
                    variances(n, q, 0)
                newton1(m, 0)
                if has_n:
                    rope_sum(n)
                newton1(m, 1)
                newton1(m, 2)
                if has_n:
                    rms_norm(n)
                    variances(n, q, 1)
                if has_j:
                    router_weights(j, p, 2)
                if has_n:
                    stack_low(n)
                    stack_k(n)
                    stack_q(n)
                if has_j:
                    router_weights(j, p, 3)
                    router_weights(j, p, 4)
                if has_n:
                    root2_input(n, q)
                if has_j:
                    combine(j, p, 0, 0)
                    combine(j, p, 0, 1)
                if has_h:
                    output_norm(h, q)
                if has_n:
                    newton2(n, 0)
                if has_m:
                    input_norm(m, p)
                if has_n:
                    newton2(n, 1)

            setup()
            batches(dve, batch, -2, 1)

        @block.scalar
        def _(act):
            a = nc.scalar
            a.preload_act_table_set("natural_log_exp_and_others")

            def roots1(m, k):
                if k == 0:
                    act.wait_ge(s_root1_in.sem, s_root1_in.at(m, 1))
                    if exists(m - 1):
                        act.wait_ge(s_ms.sem, s_ms.at(m - 1, 2))
                    a.activation(root1_ln[:], root1_in[:], ACT.Ln).then_inc(s_root1_ln.sem, 1)
                else:
                    act.wait_ge(s_root1_ln.sem, s_root1_ln.at(m, 1))
                    a.activation(root1_r[:], root1_ln[:], ACT.Exp, scale=-0.5).then_inc(s_root1_r.sem, 1)

            def xt_high(n, p):
                act.wait_ge(s_xt.sem, s_xt.at(n, 1))
                if s_hid.due(n - 2, NG):
                    act.wait_ge(s_hid.sem, s_hid.at(n - 2, NG))
                a.activation(xt_h[p][:], ps_a[:, 0:SEQ], ACT.Copy).then_inc(s_xt_h.sem, 1)

            def squares(n):
                act.wait_ge(s_qk.sem, s_qk.at(n, NT))
                a.activation(qk_sq[:], qk[:], ACT.Square).then_inc(s_qk_sq.sem, 1)

            def roots2(n, k):
                if k == 0:
                    act.wait_ge(s_root2_in.sem, s_root2_in.at(n, 1))
                    a.activation(root2_ln[:], root2_in[:], ACT.Ln).then_inc(s_root2_ln.sem, 1)
                else:
                    act.wait_ge(s_root2_ln.sem, s_root2_ln.at(n, 1))
                    a.activation(root2_r[:], root2_ln[:], ACT.Exp, scale=-0.5).then_inc(s_root2_r.sem, 1)

            def x_high(n, p):
                act.wait_ge(s_xn.sem, s_xn.at(n, NT))
                if s_x_low2.due(n - 1, 1):
                    act.wait_ge(s_x_low2.sem, s_x_low2.at(n - 1, 1))
                a.activation(x_hi[:], xn[p][:], ACT.Copy).then_inc(s_x_high.sem, 1)

            def high_half(n):
                act.wait_ge(s_qk_r.sem, s_qk_r.at(n, 1))
                if s_stack_ps.due(n - 1, 2):
                    act.wait_ge(s_stack_ps.sem, s_stack_ps.at(n - 1, 2))
                a.activation(stack[:].rearrange("p t k h s d -> p (t k h) s d")[:, :, 0, :],
                             qk_r[:].rearrange("p (h d) -> p h d", d=DH), ACT.Copy).then_inc(s_high.sem, 1)

            def take_stacks(n, p, k):
                act.wait_ge(s_stack_ps.sem, s_stack_ps.at(n, k + 1))
                if k == 0 and s_scores.due(n - 2, 2 * NG):
                    act.wait_ge(s_scores.sem, s_scores.at(n - 2, 2 * NG))
                a.activation(qk_t[p][:, k * NG:(k + 1) * NG, :].rearrange("p g s -> p (g s)"),
                             ps_a[:].bitcast(F16), ACT.Copy).then_inc(s_qk_t.sem, 1)

            def take_std(n, p):
                act.wait_ge(s_std_ps.sem, s_std_ps.at(n, 1))
                if s_hid.due(n - 2, NG):
                    act.wait_ge(s_hid.sem, s_hid.at(n - 2, NG))
                a.activation(std_t[p][0:96, :], ps_a[0:96, 0:SEQ], ACT.Copy).then_inc(s_std_t.sem, 1)

            def gates(n):
                act.wait_ge(s_lg.sem, s_lg.at(n, 4))
                a.activation(gate[:], lg3[:], ACT.Exp).then_inc(s_gate.sem, 1)

            def square_scores(j, g, half):
                act.wait_ge(s_scores.sem, s_scores.at(j, 2 * g + half + 1))
                if half == 0 and s_pv.due(j, g - 1):
                    act.wait_ge(s_pv.sem, s_pv.at(j, g - 1))
                heads = slice(2 * half, 2 * half + 2)
                a.activation(probs[g % 2][:, heads, :], ps_s[:, heads, 0:3 * 128], ACT.Square,
                             scale=1.0 / (DH * QK_SCALE * QK_SCALE)).then_inc(s_probs.sem, 1)

            def relu(j, e):
                act.wait_ge(s_hid.sem, s_hid.at(j, e + 1))
                if s_expert.due(j, e - 1):
                    act.wait_ge(s_expert.sem, s_expert.at(j, e - 1))
                a.activation(hid_t[e % 2][:], ps_h[:], ACT.Relu).then_inc(s_relu.sem, 1)

            def take_z(j):
                act.wait_ge(s_pv.sem, s_pv.at(j, NG))
                if s_attn.due(j - 1, 1):
                    act.wait_ge(s_attn.sem, s_attn.at(j - 1, 1))
                a.activation(z_t[:], ps_z[:, 0:SEQ], ACT.Copy).then_inc(s_z_t.sem, 1)

            def batch(j, p):
                h, n, m, q = j - 1, j + 1, j + 2, 1 - p
                has_h, has_j, has_n, has_m = exists(h), exists(j), exists(n), exists(m)
                if has_j:
                    take_stacks(j, p, 1)
                if has_h:
                    relu(h, 3)
                    take_z(h)
                if has_j:
                    take_std(j, p)
                    gates(j)
                if has_n:
                    xt_high(n, q)
                if has_j:
                    square_scores(j, 0, 0)
                    square_scores(j, 0, 1)
                    relu(j, 0)
                if has_n:
                    squares(n)
                if has_j:
                    relu(j, 1)
                    square_scores(j, 1, 0)
                roots1(m, 0)
                roots1(m, 1)
                if has_j:
                    square_scores(j, 1, 1)
                    square_scores(j, 2, 0)
                    square_scores(j, 2, 1)
                if has_n:
                    high_half(n)
                if has_j:
                    relu(j, 2)
                    square_scores(j, 3, 0)
                    square_scores(j, 3, 1)
                if has_n:
                    roots2(n, 0)
                    roots2(n, 1)
                    take_stacks(n, q, 0)
                if has_m:
                    x_high(m, p)

            batches(act, batch, -2, 1)

        @block.gpsimd
        def _(pool):
            g_ = nc.gpsimd

            def mask(j, g, half):
                pool.wait_ge(s_probs.sem, s_probs.at(j, 2 * g + half + 1))
                pool.nop(nofuse=True)
                diagonal = probs[g % 2][:, 2 * half:2 * half + 2, 0:2 * 128]
                g_.affine_select(out=diagonal, in_=diagonal, compare_op=ALU.is_ge, fill=0.0, base=0,
                                 pattern=[[0, 2], [0, 2], [1, 128]],
                                 channel_multiplier=-1).then_inc(s_masked.sem, 1)

            def rope_sin(n):
                pool.wait_ge(s_qk.sem, s_qk.at(n, NT))
                pairs = "p (t h a two) -> p t h a two"
                g_.tensor_tensor(rope2[:].rearrange(pairs, t=NT, a=DH // 2, two=2),
                                 qk[:].rearrange("p t (h a two) -> p t h a two", a=DH // 2, two=2)[:, :, :, :, ::-1],
                                 sin_t[:].rearrange("p t (a two) -> p t a two", two=2).unsqueeze(2)
                                 .to_broadcast([128, NT, 2 * HEADS, DH // 2, 2]),
                                 ALU.mult).then_inc(s_rope2.sem, 1)

            def residual(n, p, k):
                if k == 0:
                    pool.wait_ge(s_xn.sem, s_xn.at(n, NT))
                    if s_base1.due(n - 1, 1):
                        pool.wait_ge(s_base1.sem, s_base1.at(n - 1, 1))
                    g_.tensor_tensor(base0[:], x_in[p][:], xn[p][:], ALU.add).then_inc(s_base0.sem, 1)
                else:
                    pool.wait_ge(s_base0.sem, s_base0.at(n, 1))
                    if s_base2.due(n - 2, 1):
                        pool.wait_ge(s_base2.sem, s_base2.at(n - 2, 1))
                    g_.tensor_tensor(base1[p][:], base0[:], on_gb[:, 1:2, :].to_broadcast([128, NT, D]),
                                     ALU.add).then_inc(s_base1.sem, 1)

            def finish(j, p, k):
                if k == 0:
                    pool.wait_ge(s_ffn_n.sem, s_ffn_n.at(j, NT))
                    g_.tensor_tensor(ffn_g[:], ffn_n[:], on_gb[:, 0:1, :].to_broadcast([128, NT, D]),
                                     ALU.mult).then_inc(s_ffn_g.sem, 1)
                else:
                    pool.wait_ge(s_ffn_g.sem, s_ffn_g.at(j, 1))
                    pool.wait_ge(s_base2.sem, s_base2.at(j, 1))
                    if y_stored[p].due(j - 2 - p, 16):
                        pool.wait_ge(y_stored[p].sem, y_stored[p].at(j - 2 - p, 16))
                    g_.tensor_tensor(y[p][:], ffn_g[:], base2[:], ALU.add).then_inc(s_y.sem, 1)

            def batch(j, p):
                h, n, m, q = j - 1, j + 1, j + 2, 1 - p
                has_h, has_j, has_n, has_m = exists(h), exists(j), exists(n), exists(m)
                if has_n:
                    residual(n, q, 0)
                if has_j:
                    mask(j, 0, 0)
                    mask(j, 0, 1)
                if has_n:
                    rope_sin(n)
                if has_j:
                    mask(j, 1, 0)
                if has_n:
                    residual(n, q, 1)
                if has_j:
                    mask(j, 1, 1)
                    mask(j, 2, 0)
                    mask(j, 2, 1)
                    mask(j, 3, 0)
                    mask(j, 3, 1)
                if has_h:
                    finish(h, q, 0)
                    finish(h, q, 1)

            pool.wait_ge(loaded.sem, 16 * LOADS)
            batches(pool, batch, -2, 1)

        @block.tensor
        def _(pe):
            t_ = nc.tensor

            def setup():
                pe.wait_ge(loaded.sem, 16 * LOADS)
                for n in range(4):
                    t_.transpose(ps_s[:, 0, n * D:(n + 1) * D], w_raw[:, n, :], ident[:])
                t_.transpose(ps_s[:, 1, 0:EXPERTS], router_raw[:],
                             ident[0:EXPERTS, 0:EXPERTS]).then_inc(p_setup.sem, 1)
                pe.wait_ge(v_setup.sem, V_CENTRED)
                for c in range(EXPERTS * CH):
                    last = t_.transpose(ps_s[:, 2 + c // 4, (c % 4) * D:(c % 4 + 1) * D],
                                        w1_c[:].rearrange("p e h -> p (e h)")[:, c * 128:(c + 1) * 128], ident[:])
                last.then_inc(p_setup.sem, 1)
                pe.wait_ge(v_setup.sem, V_W1_CT)
                for e in range(EXPERTS):
                    for c in range(CH):
                        w_t = w1_ct[:, e * CH + c, :]
                        last = t_.matmul(ps_h[:, e * D:(e + 1) * D], w_t, w_t, start=(c == 0), stop=(c == CH - 1))
                last.then_inc(p_setup.sem, 1)
                t_.matmul(ps_o[:, 0:EXPERTS], rn_b_all[:], router_t[:], start=True,
                          stop=True).then_inc(p_setup.sem, 1)
                pe.wait_ge(v_setup.sem, V_DONE)

            def three_passes(dst, stationary, moving, start=True, stop=True):
                (sh, sl), (mh, ml) = stationary, moving
                t_.matmul(dst, sh, mh, start=start, stop=False)
                t_.matmul(dst, sh, ml, start=False, stop=False)
                return t_.matmul(dst, sl, mh, start=False, stop=stop)

            def x_halves(p, t):
                cols = slice(t * 128, (t + 1) * 128)
                return xt_h[p][:, cols], xt_l[p][:, cols]

            def transpose_x(n, p):
                pe.wait_ge(s_xn.sem, s_xn.at(n, NT))
                if s_std_t.due(n - 1, 1):
                    pe.wait_ge(s_std_t.sem, s_std_t.at(n - 1, 1))
                for t in range(NT):
                    last = t_.transpose(ps_a[:, t * 128:(t + 1) * 128], xn[p][:, t, :], ident[:])
                last.then_inc(s_xt.sem, 1)

            def project(n, p, t):
                if t == 0:
                    pe.wait_ge(s_xt_l.sem, s_xt_l.at(n, 1))
                else:
                    pe.wait_ge(s_logits0.sem, s_logits0.at(n, t))
                three_passes(ps_a[:, 0:PROJ], x_halves(p, t), (proj_h[:], proj_l[:])).then_inc(s_proj.sem, 1)

            def gram(n, p, t):
                if t == 0:
                    pe.wait_ge(s_logits0.sem, s_logits0.at(n, NT))
                else:
                    pe.wait_ge(s_var.sem, s_var.at(n, t * EXPERTS))
                x_high_t = x_halves(p, t)[0]
                t_.matmul(ps_a[:], x_high_t, gram_h[:], start=True, stop=False)
                t_.matmul(ps_a[:], x_high_t, gram_l[:], start=False, stop=True).then_inc(s_gram.sem, 1)

            def transpose_stacks(n, k):
                if k == 0:
                    pe.wait_ge(s_stack.sem, s_stack.at(n, 2))
                    pe.wait_ge(s_var.sem, s_var.at(n, NV))
                else:
                    pe.wait_ge(s_qk_t.sem, s_qk_t.at(n, 1))
                dst = ps_a[:].bitcast(F16)
                for g in range(NG):
                    for t in range(NT):
                        at = g * SEQ + t * 128
                        rows = stack[:, t, k, g * NC:(g + 1) * NC].rearrange("p h s d -> p (h s d)")
                        last = t_.transpose(dst[:, at:at + 128], rows, ident16[:])
                last.then_inc(s_stack_ps.sem, 1)

            def transpose_std(n):
                pe.wait_ge(s_std_cols.sem, s_std_cols.at(n, 3))
                pe.wait_ge(s_qk_t.sem, s_qk_t.at(n, 2))
                for t in range(NT):
                    last = t_.transpose(ps_a[0:96, t * 128:(t + 1) * 128], std_cols[:, t, :], ident[:])
                last.then_inc(s_std_ps.sem, 1)

            def scores(j, p, g, half):
                if g == 0 and half == 0:
                    pe.wait_ge(s_qk_t.sem, s_qk_t.at(j, 2))
                if s_probs.due(j, 2 * g - 1 + half):
                    pe.wait_ge(s_probs.sem, s_probs.at(j, 2 * g - 1 + half))
                heads = range(2 * half, 2 * half + 2)
                for c in heads:
                    r = slice(32 * c, 32 * c + 32)
                    t_.matmul(ps_s[:, c, 128:384], qk_t[p][r, NG + g, 0:128], qk_t[p][r, g, :], start=True, stop=True)
                for c in heads:
                    r = slice(32 * c, 32 * c + 32)
                    last = t_.matmul(ps_s[:, c, 0:128], qk_t[p][r, NG + g, 128:256], qk_t[p][r, g, 128:256],
                                     start=True, stop=True)
                last.then_inc(s_scores.sem, 1)

            def weigh_values(j, p, g):
                pe.wait_ge(s_masked.sem, s_masked.at(j, 2 * g + 2))
                if g == 0:
                    if s_z_t.due(j - 1, 1):
                        pe.wait_ge(s_z_t.sem, s_z_t.at(j - 1, 1))
                for t in range(NT):
                    for c in range(NC):
                        at = (g * NC + c) * 32
                        q0 = 0 if t == 0 else 128
                        cols = slice(128, 384) if t == 0 else slice(0, 128)
                        last = t_.matmul(ps_z[32 * c:32 * c + 32, q0:SEQ], vz[p][:, t, at:at + 32],
                                         probs[g % 2][:, c, cols], start=(g == 0 and t == 0),
                                         stop=(g == NG - 1 and t == NT - 1), skip_group_check=True)
                last.then_inc(s_pv.sem, 1)

            def hidden(j, p, e):
                if e == 0:
                    pe.wait_ge(s_std_t.sem, s_std_t.at(j, 1))
                if s_relu.due(j, e):
                    pe.wait_ge(s_relu.sem, s_relu.at(j, e))
                for c in range(CH):
                    cols = slice((e * CH + c) * 128, (e * CH + c + 1) * 128)
                    dst = ps_h[:, c * SEQ:(c + 1) * SEQ]
                    three_passes(dst, (w1_h[:, cols], w1_l[:, cols]), (xt_h[p][:], xt_l[p][:]), stop=False)
                    last = t_.matmul(dst, b_rows[:, cols], std_t[p][:], start=False, stop=True)
                last.then_inc(s_hid.sem, 1)

            def expert_out(j, p, e):
                pe.wait_ge(s_relu.sem, s_relu.at(j, e + 1))
                if e == 0:
                    if s_base2.due(j - 1, 1):
                        pe.wait_ge(s_base2.sem, s_base2.at(j - 1, 1))
                else:
                    pe.wait_ge(s_acc.sem, s_acc.at(j, e * NT))
                for t in range(NT):
                    for c in range(CH):
                        at = c * SEQ + t * 128
                        last = t_.matmul(ps_o[:, t * D:(t + 1) * D], hid_t[e % 2][:, at:at + 128],
                                         w2_sb[:, e * CH + c, :], start=(c == 0), stop=(c == CH - 1))
                last.then_inc(s_expert.sem, 1)

            def attention_out(j):
                pe.wait_ge(s_z_t.sem, s_z_t.at(j, 1))
                pe.wait_ge(s_acc.sem, s_acc.at(j, (EXPERTS - 1) * NT))
                for t in range(NT):
                    at = (NT + t) * D
                    last = t_.matmul(ps_o[:, at:at + D], z_t[:, t * 128:(t + 1) * 128], wo_t[:],
                                     start=True, stop=True)
                last.then_inc(s_attn.sem, 1)

            def batch(j, p):
                h, n, m, q = j - 1, j + 1, j + 2, 1 - p
                has_h, has_j, has_n, has_m = exists(h), exists(j), exists(n), exists(m)
                if has_h:
                    weigh_values(h, q, 3)
                    expert_out(h, q, 2)
                if has_j:
                    transpose_std(j)
                    scores(j, p, 0, 0)
                    scores(j, p, 0, 1)
                if has_n:
                    transpose_x(n, q)
                if has_h:
                    expert_out(h, q, 3)
                    attention_out(h)
                if has_n:
                    project(n, q, 0)
                if has_j:
                    hidden(j, p, 0)
                if has_n:
                    project(n, q, 1)
                if has_j:
                    scores(j, p, 1, 0)
                    hidden(j, p, 1)
                    weigh_values(j, p, 0)
                if has_n:
                    gram(n, q, 0)
                if has_j:
                    scores(j, p, 1, 1)
                    expert_out(j, p, 0)
                    scores(j, p, 2, 0)
                if has_n:
                    gram(n, q, 1)
                if has_j:
                    scores(j, p, 2, 1)
                    hidden(j, p, 2)
                    scores(j, p, 3, 0)
                    weigh_values(j, p, 1)
                    scores(j, p, 3, 1)
                    hidden(j, p, 3)
                if has_n:
                    transpose_stacks(n, 0)
                if has_j:
                    weigh_values(j, p, 2)
                    expert_out(j, p, 1)
                if has_n:
                    transpose_stacks(n, 1)

            setup()
            batches(pe, batch, -2, 1)


def kernel(**inputs):
    import concourse.bacc as bacc
    from concourse.bass_utils import run_bass_kernel_spmd

    names = ["x", "Wq", "bq", "Wk", "bk", "Wv", "bv", "Wo", "norm_w"]
    names = [f"L0_attn_{n}" for n in names]
    names += [f"L0_ffn_{n}" for n in ("router_w", "rn_g", "rn_b", "w1", "ln_g", "ln_b", "w2", "on_g", "on_b")]
    inv_freq = (1.0 / np.float32(10000.0) ** (np.arange(0, DH, 2, dtype=np.float32) / np.float32(DH))).astype(np.float32)
    freqs = np.outer(np.arange(SEQ, dtype=np.float32), inv_freq).astype(np.float32)
    emb = np.concatenate([freqs, freqs], -1)
    sign = np.where(np.arange(DH) % 2 == 0, -1.0, 1.0).astype(np.float32)
    rope_c = np.stack([np.cos(emb), sign * np.sin(emb)]).astype(np.float32)
    rope_c = np.ascontiguousarray(rope_c.reshape(2, NT, 128, DH).transpose(2, 0, 1, 3))
    consts = {
        "identity": np.eye(128, dtype=np.float32),
        "rope": rope_c,
        "earlier": np.tril(np.ones((EXPERTS, EXPERTS), np.float32), -1),
    }
    nc = bacc.Bacc("TRN2", target_bir_lowering=False, num_devices=1)
    arrays, args = {}, []
    for name, a in [(n, np.ascontiguousarray(inputs[n])) for n in names] + list(consts.items()):
        arrays[f"in_{name}"] = a
        args.append(nc.dram_tensor(f"in_{name}", a.shape, mybir.dt.from_np(a.dtype), kind="ExternalInput").ap())
    out = nc.dram_tensor("out", (B, SEQ, D), F32, kind="ExternalOutput").ap()
    build(nc, *args, out)
    result = run_bass_kernel_spmd(nc, [arrays], core_ids=[0])
    return result.results[0]["out"]
```

```python
from contextlib import ExitStack

import numpy as np

import concourse.bass as bass
from concourse import mybir

F32 = mybir.dt.float32
F32R = mybir.dt.float32r
F16 = mybir.dt.float16
ALU = mybir.AluOpType
ACT = mybir.ActivationFunctionType
AX_X = mybir.AxisListType.X

B, SEQ, D = 32, 256, 128
NT = SEQ // 128
HEADS, DH = 16, 8
NG = 4
NC = HEADS // NG
EXPERTS, HID = 4, 256
CH = HID // 128
SLOTS = 4
QKV = 3 * D
PROJ = QKV + EXPERTS
EPS_LN = 1e-5
EPS_RMS = float(np.finfo(np.float32).eps)
EPS_GATE = 1e-8
ROPE_AT = 128
EARLIER_AT = ROPE_AT + 2 * NT * DH
BLOCK_AT = EARLIER_AT + EXPERTS * EXPERTS
CONSTS = BLOCK_AT + EXPERTS
QK_SCALE = 16.0


class Signal:

    def __init__(self, sem, per):
        self.sem, self.per = sem, per

    def at(self, j, n):
        return j * self.per + n

    def due(self, j, n):
        value = self.at(j, n)
        return not isinstance(value, int) or value > 0


def build(nc, x, wq, bq, wk, bk, wv, bv, wo, norm_w, router_w, rn_g, rn_b, w1, ln_g, ln_b, w2,
          on_g, on_b, consts_c, out):
    ctx = ExitStack()
    with ctx:
        def sb(name, shape, dt=F32):
            return ctx.enter_context(nc.sbuf_tensor(name, shape, dt))

        def ps(name, shape):
            return ctx.enter_context(nc.psum_tensor(name, shape, F32))

        def signal(name, per):
            return Signal(ctx.enter_context(nc.semaphore(name)), per)

        consts = sb("consts", [128, CONSTS])
        ident = consts[:, 0:128]
        rope = consts[:, ROPE_AT:EARLIER_AT].rearrange("p (k t d) -> p k t d", k=2, t=NT)
        earlier = consts[:, EARLIER_AT:BLOCK_AT].rearrange("p (i j) -> p i j", i=EXPERTS)
        own_block = consts[:, BLOCK_AT:CONSTS]
        ident16 = sb("ident16", [128, 128], F16)
        w_raw = sb("w_raw", [128, 4, D])
        bias_raw = sb("bias_raw", [128, 3, D])
        bias = sb("bias", [128, QKV])
        router_raw = sb("router_raw", [EXPERTS, D])
        rn_cols = sb("rn_cols", [128, 2])
        w1_raw = sb("w1_raw", [128, EXPERTS, HID])
        w1_c = sb("w1_c", [128, EXPERTS, HID])
        w1_g = sb("w1_g", [128, EXPERTS, HID])
        w1_mean = sb("w1_mean", [128, EXPERTS])
        w1_ct = sb("w1_ct", [128, EXPERTS * CH, D])
        ln_g_all = sb("ln_g_all", [128, EXPERTS, HID])
        b_raw = sb("b_raw", [128, EXPERTS, HID])
        b_own = sb("b_own", [128, EXPERTS, HID])
        w2_sb = sb("w2_sb", [128, EXPERTS * CH, D])
        on_gb = sb("on_gb", [128, 2, D])
        nw = sb("nw", [128, DH])
        nw_m = sb("nw_m", [128, 4])
        nw_s = sb("nw_s", [128, DH])
        proj_h = sb("proj_h", [128, PROJ], F32R)
        proj_l = sb("proj_l", [128, PROJ], F32R)
        router_t = sb("router_t", [128, EXPERTS])
        router_g = sb("router_g", [128, EXPERTS])
        router_b = sb("router_b", [128, EXPERTS])
        wo_t = sb("wo_t", [128, D])
        w1_h = sb("w1_h", [128, EXPERTS * HID], F32R)
        w1_l = sb("w1_l", [128, EXPERTS * HID], F32R)
        gram_h = sb("gram_h", [128, EXPERTS * D], F32R)
        gram_l = sb("gram_l", [128, EXPERTS * D], F32R)
        b_rows = sb("b_rows", [128, EXPERTS * HID], F32R)
        cos_t = sb("cos_t", [128, NT, DH])
        sin_t = sb("sin_t", [128, NT, DH])

        x_in = [sb(f"x_in{p}", [128, NT, D]) for p in range(2)]
        xn = [sb(f"xn{p}", [128, NT, D]) for p in range(2)]
        x_hi = sb("x_hi", [128, NT, D], F32R)
        x_low2 = [sb(f"x_low2{p}", [128, NT, D]) for p in range(2)]
        xt_h = [sb(f"xt_h{p}", [128, SEQ], F32R) for p in range(2)]
        xt_l = [sb(f"xt_l{p}", [128, SEQ], F32R) for p in range(2)]
        vz = [sb(f"vz{p}", [128, NT, NG * 136]) for p in range(2)]
        qk_t = [sb(f"qk_t{p}", [128, 2 * NG, SEQ], F16) for p in range(2)]
        std_t = [sb(f"std_t{p}", [128, SEQ], F32R) for p in range(2)]
        scale_e = [sb(f"scale_e{p}", [128, NT, EXPERTS]) for p in range(2)]
        stats = sb("stats", [128, 2 * NT, 6])
        mean_var = sb("mean_var", [128, 2 * NT, 2])
        NM = NT * 2 * HEADS
        root1_in = sb("root1_in", [128, NM + 2 * NT])
        root1_ln = sb("root1_ln", [128, NM + 2 * NT])
        root1_r = sb("root1_r", [128, NM + 2 * NT])
        root1_a = sb("root1_a", [128, NM + 2 * NT])
        root1_b = sb("root1_b", [128, NM + 2 * NT])
        root1 = sb("root1", [128, NM + 2 * NT])
        rms, rstd_f, rstd_x = root1[:, 0:NM], root1[:, NM:NM + NT], root1[:, NM + NT:NM + 2 * NT]
        qk = sb("qk", [128, NT, 2 * D])
        logits0 = sb("logits0", [128, NT, EXPERTS])
        qk_sq = sb("qk_sq", [128, NT, 2 * D])
        ms_sum = sb("ms_sum", [128, NM])
        rope_qk = sb("rope_qk", [128, NT * 2 * D])
        rope1 = sb("rope1", [128, NT * 2 * D])
        rope2 = sb("rope2", [128, NT * 2 * D])
        qk_r = sb("qk_r", [128, NT * 2 * D])
        stack = sb("stack", [128, NT, 2, HEADS, SLOTS, DH], F16)
        NV = NT * EXPERTS
        scrap = sb("scrap", [128, NV, D])
        var = [sb(f"var{p}", [128, NV + NT]) for p in range(2)]
        rt1 = sb("rt1", [128, NT])
        root2_in = sb("root2_in", [128, NV + NT])
        root2_ln = sb("root2_ln", [128, NV + NT])
        root2_r = sb("root2_r", [128, NV + NT])
        root2_a = sb("root2_a", [128, NV + NT])
        root2_b = sb("root2_b", [128, NV + NT])
        root2 = sb("root2", [128, NV + NT])
        std = sb("std", [128, NV])
        std_cols = sb("std_cols", [128, NT, 96])
        lg2 = sb("lg2", [128, NT, EXPERTS])
        lg_max = sb("lg_max", [128, NT])
        lg3 = sb("lg3", [128, NT, EXPERTS])
        gate = sb("gate", [128, NT, EXPERTS])
        gate_sum = sb("gate_sum", [128, NT])
        ahead = sb("ahead", [128, NT, EXPERTS, EXPERTS])
        tied = sb("tied", [128, NT, EXPERTS, EXPERTS])
        beaten = sb("beaten", [128, NT, EXPERTS, EXPERTS])
        rank = sb("rank", [128, NV])
        chosen = sb("chosen", [128, NT, EXPERTS])
        chosen_sum = sb("chosen_sum", [128, NT])
        gate_den = sb("gate_den", [128, NT])
        gate_inv = sb("gate_inv", [128, NT])
        probs = [sb(f"probs{b}", [128, NC, 3 * 128]) for b in range(2)]
        hid_t = [sb(f"hid_t{b}", [128, CH * SEQ]) for b in range(2)]
        acc = [sb(f"acc{p}", [128, NT, D]) for p in range(2)]
        z_t = sb("z_t", [128, SEQ])
        ffn_n = sb("ffn_n", [128, NT, D])
        ffn_g = sb("ffn_g", [128, NT, D])
        base0 = sb("base0", [128, NT, D])
        base1 = [sb(f"base1_{p}", [128, NT, D]) for p in range(2)]
        base2 = sb("base2", [128, NT, D])
        y = [sb(f"y{p}", [128, NT, D]) for p in range(2)]

        ps_s = ps("ps_s", [128, NC, 512])
        ps_z = ps("ps_z", [128, 512])
        ps_h = ps("ps_h", [128, 512])
        ps_o = ps("ps_o", [128, 512])
        ps_a = ps("ps_a", [128, 512])

        loaded_w1 = signal("loaded_w1", 16 * 2)
        loaded_proj = signal("loaded_proj", 16 * 7)
        loaded_nw = signal("loaded_nw", 16)
        loaded_bias = signal("loaded_bias", 16 * 3)
        loaded_ln = signal("loaded_ln", 16)
        loaded_b = signal("loaded_b", 16 * 3)
        loaded_out = signal("loaded_out", 16 * 3)
        v_chain = signal("v_chain", 1)
        b_zeroed = signal("b_zeroed", 1)
        vz_zeroed = signal("vz_zeroed", 1)
        w1_centred = signal("w1_centred", 1)
        w1_ct_ps = signal("w1_ct_ps", 2)
        w1_ct_taken = signal("w1_ct_taken", 2)
        weights_ps = signal("weights_ps", 1)
        router_taken = signal("router_taken", 1)
        gram_ps = signal("gram_ps", 1)
        gram_high = signal("gram_high", 1)
        gram_done = signal("gram_done", 1)
        router_b_ps = signal("router_b_ps", 1)
        proj_done = signal("proj_done", 1)
        w1_scaled = signal("w1_scaled", 1)
        w1_high = signal("w1_high", 1)
        w1_done = signal("w1_done", 1)
        b_masked = signal("b_masked", 1)
        b_high = signal("b_high", 1)
        b_done = signal("b_done", 1)
        ident16_done = signal("ident16_done", 1)
        x_loaded = [signal(f"x_loaded{p}", 16 // 2) for p in range(2)]
        y_stored = [signal(f"y_stored{p}", 16 // 2) for p in range(2)]
        s_stats_x = signal("s_stats_x", NT)
        s_stats_f = signal("s_stats_f", NT)
        s_mean_var_x = signal("s_mean_var_x", NT)
        s_mean_var_f = signal("s_mean_var_f", NT)
        s_root1_in = signal("s_root1_in", 1)
        s_root1_ln = signal("s_root1_ln", 1)
        s_root1_r = signal("s_root1_r", 1)
        s_root1 = signal("s_root1", 3)
        s_xn = signal("s_xn", NT)
        s_xt = signal("s_xt", 1)
        s_xt_h = signal("s_xt_h", 1)
        s_xt_l = signal("s_xt_l", 1)
        s_proj = signal("s_proj", NT)
        s_qk = signal("s_qk", NT)
        s_v = signal("s_v", NT)
        s_logits0 = signal("s_logits0", NT)
        s_qk_sq = signal("s_qk_sq", 1)
        s_ms = signal("s_ms", 2)
        s_rope_qk = signal("s_rope_qk", 1)
        s_rope1 = signal("s_rope1", 1)
        s_rope2 = signal("s_rope2", 1)
        s_qk_r = signal("s_qk_r", 1)
        s_high = signal("s_high", 1)
        s_low = signal("s_low", 1)
        s_stack = signal("s_stack", 2)
        s_stack_ps = signal("s_stack_ps", 2)
        s_qk_t = signal("s_qk_t", 2)
        s_gram = signal("s_gram", NT)
        s_var = signal("s_var", NV)
        s_router_var = signal("s_router_var", 2)
        s_root2_in = signal("s_root2_in", 1)
        s_root2_ln = signal("s_root2_ln", 1)
        s_root2_r = signal("s_root2_r", 1)
        s_root2 = signal("s_root2", 3)
        s_std = signal("s_std", 1)
        s_std_cols = signal("s_std_cols", 3)
        s_std_ps = signal("s_std_ps", 1)
        s_std_t = signal("s_std_t", 1)
        s_lg = signal("s_lg", 4)
        s_gate = signal("s_gate", 1)
        s_gate_sum = signal("s_gate_sum", 1)
        s_rank = signal("s_rank", 4)
        s_weight = signal("s_weight", 4)
        s_scale_e = signal("s_scale_e", NT)
        s_scores = signal("s_scores", 2 * NG)
        s_probs = signal("s_probs", 2 * NG)
        s_masked = signal("s_masked", 2 * NG)
        s_pv = signal("s_pv", NG)
        s_hid = signal("s_hid", NG)
        s_relu = signal("s_relu", NG)
        s_expert = signal("s_expert", NG)
        s_acc = signal("s_acc", NG * NT)
        s_z_t = signal("s_z_t", 1)
        s_attn = signal("s_attn", 1)
        s_base0 = signal("s_base0", 1)
        s_base1 = signal("s_base1", 1)
        s_base2 = signal("s_base2", 1)
        s_ffn_n = signal("s_ffn_n", NT)
        s_ffn_g = signal("s_ffn_g", 1)
        s_y = signal("s_y", 1)

        s_x_high = signal("s_x_high", 1)
        s_x_low2 = signal("s_x_low2", 1)

        x_v = x.rearrange("b (t p) d -> p (b t) d", p=128)
        out_v = out.rearrange("b (t p) d -> p (b t) d", p=128)
        block = ctx.enter_context(nc.Block())

        def batches(eng, batch, setup, straight_after, tail=2):
            for j in range(-2, 4):
                if j in setup:
                    setup[j]()
                batch(j, j % 2)
            with eng.Fori(2, (B - tail) // 2) as i:
                for p in range(2):
                    batch(i * 2 + p, p)
            for j in range(B - tail, B + straight_after):
                batch(j, j % 2)

        def known(j):
            return isinstance(j, int)

        def exists(j):
            return not known(j) or 0 <= j < B

        @block.sync
        def _(sp):
            def load(signal, dst, src):
                sp.dma_start(dst, src).then_inc(signal.sem, 16)

            load(loaded_nw, nw[:], norm_w.partition_broadcast(128))
            load(loaded_w1, consts[:], consts_c)
            load(loaded_w1, w1_raw[:], w1.rearrange("e d h -> d e h"))
            load(x_loaded[0], x_in[0][:], x_v[:, 0:NT, :])
            load(loaded_ln, ln_g_all[:], ln_g.partition_broadcast(128))
            for n, w in enumerate((wq, wk, wv, wo)):
                load(loaded_proj, w_raw[:, n, :], w)
            load(loaded_proj, router_raw[:], router_w)
            load(loaded_proj, rn_cols[:, 0:1], rn_g.unsqueeze(1))
            load(loaded_proj, rn_cols[:, 1:2], rn_b.unsqueeze(1))
            for n, b in enumerate((bq, bk, bv)):
                load(loaded_bias, bias_raw[:, n, :], b.partition_broadcast(128))
            load(x_loaded[1], x_in[1][:], x_v[:, NT:2 * NT, :])
            sp.wait_ge(b_zeroed.sem, 1)
            for quadrant in range(3):
                r = 32 * quadrant
                load(loaded_b, b_raw[r:r + EXPERTS], ln_b.partition_broadcast(EXPERTS))
            load(loaded_out, on_gb[:, 0, :], on_g.partition_broadcast(128))
            load(loaded_out, on_gb[:, 1, :], on_b.partition_broadcast(128))
            load(loaded_out, w2_sb[:], w2.rearrange("e (c h) d -> h (e c) d", h=128))

            def batch(j, p):
                n, q = j + 1, 1 - p
                if exists(n) and exists(n + 2):
                    if s_base0.due(n, 1):
                        sp.wait_ge(s_base0.sem, s_base0.at(n, 1))
                    sp.dma_start(x_in[q][:], x_v[:, bass.ds((n + 2) * NT, NT), :]).then_inc(x_loaded[q].sem, 16)
                if exists(j - 1):
                    sp.wait_ge(s_y.sem, s_y.at(j - 1, 1))
                    sp.dma_start(out_v[:, bass.ds((j - 1) * NT, NT), :], y[q][:]).then_inc(y_stored[q].sem, 16)

            batches(sp, batch, {}, 1, tail=4)
            for p in range(2):
                sp.wait_ge(y_stored[p].sem, y_stored[p].at(B - 2, 16))

        @block.vector
        def _(dve):
            v = nc.vector
            chain = [0]

            def link(ins, steps=1):
                chain[0] += steps
                ins.then_inc(v_chain.sem, 1)
                dve.wait_ge(v_chain.sem, chain[0])

            def perm(ap):
                return ap.rearrange("p (c g d) -> p g c d", c=NC, g=NG)

            def rows(ap):
                return ap.rearrange("p (g c d) -> p g c d", c=NC, g=NG)

            def setup_first():
                link(v.memset(mean_var[:], 0.0))
                link(v.memset(root1_in[:], 1.0))
                link(v.memset(std_cols[:], 0.0))
                for p in range(2):
                    link(v.memset(std_t[p][:].bitcast(F32), 0.0))
                dve.wait_ge(loaded_nw.sem, loaded_nw.per)
                link(v.tensor_reduce(nw_m[:, 0:1], nw[:], AX_X, ALU.max, apply_absolute_value=True))
                link(v.tensor_scalar(nw_m[:, 0:1], nw_m[:, 0:1], 1e-30, None, ALU.max))
                link(v.reciprocal(nw_m[:, 1:2], nw_m[:, 0:1]))
                v.tensor_tensor(nw_m[:, 2:3], nw_m[:, 0:1], nw_m[:, 0:1], ALU.mult).then_inc(v_chain.sem, 1)
                link(v.tensor_scalar(nw_s[:], nw[:], nw_m[:, 1:2], QK_SCALE, ALU.mult, ALU.mult), 2)
                link(v.tensor_tensor(nw_m[:, 3:4], nw_m[:, 2:3], nw_m[:, 2:3], ALU.mult))
                dve.wait_ge(loaded_w1.sem, loaded_w1.per)
                link(v.tensor_reduce(w1_mean[:], w1_raw[:], AX_X, ALU.add))
                link(v.tensor_scalar(w1_mean[:], w1_mean[:], 1.0 / HID, None, ALU.mult))
                v.tensor_tensor(w1_c[:], w1_raw[:], w1_mean[:].unsqueeze(2).to_broadcast([128, EXPERTS, HID]),
                                ALU.subtract).then_inc(w1_centred.sem, 1)

            def setup_stage_a():
                v.tensor_tensor(cos_t[:], rope[:, 0], nw_s[:].unsqueeze(1).to_broadcast([128, NT, DH]),
                                ALU.mult).then_inc(v_chain.sem, 1)
                nw_pairs = nw_s[:].rearrange("p (a two) -> p a two", two=2)
                for t in range(NT):
                    ins = v.tensor_tensor(sin_t[:, t].rearrange("p (a two) -> p a two", two=2),
                                          rope[:, 1, t].rearrange("p (a two) -> p a two", two=2),
                                          nw_pairs[:, :, ::-1], ALU.mult)
                    if t < NT - 1:
                        ins.then_inc(v_chain.sem, 1)
                    else:
                        link(ins, 1 + NT)
                dve.wait_ge(weights_ps.sem, 1)
                v.tensor_copy(router_t[:], ps_s[:, 1, 0:EXPERTS]).then_inc(router_taken.sem, 1)
                for n in range(2):
                    v.tensor_copy(rows(proj_h[:, n * D:(n + 1) * D]),
                                  perm(ps_s[:, 0, n * D:(n + 1) * D])).then_inc(v_chain.sem, 1)
                link(v.tensor_copy(proj_h[:, 2 * D:QKV], ps_s[:, 0, 2 * D:3 * D]), 3)
                for n in range(2):
                    v.tensor_tensor(rows(proj_l[:, n * D:(n + 1) * D]), perm(ps_s[:, 0, n * D:(n + 1) * D]),
                                    rows(proj_h[:, n * D:(n + 1) * D]).bitcast(F32),
                                    ALU.subtract).then_inc(v_chain.sem, 1)
                link(v.tensor_tensor(proj_l[:, 2 * D:QKV], ps_s[:, 0, 2 * D:3 * D],
                                     proj_h[:, 2 * D:QKV].bitcast(F32), ALU.subtract), 3)
                dve.wait_ge(router_taken.sem, 1)
                link(v.tensor_scalar(router_g[:], router_t[:], rn_cols[:, 0:1], None, ALU.mult))
                link(v.tensor_copy(proj_h[:, QKV:PROJ], router_g[:]))
                link(v.tensor_tensor(proj_l[:, QKV:PROJ], router_g[:], proj_h[:, QKV:PROJ].bitcast(F32),
                                     ALU.subtract))
                v.tensor_scalar(wo_t[:], ps_s[:, 0, 3 * D:4 * D], nw_m[:, 3:4], None,
                                ALU.mult).then_inc(proj_done.sem, 1)
                dve.wait_ge(loaded_bias.sem, loaded_bias.per)
                for n in range(2):
                    v.tensor_copy(rows(bias[:, n * D:(n + 1) * D]), perm(bias_raw[:, n, :])).then_inc(v_chain.sem, 1)
                link(v.tensor_copy(bias[:, 2 * D:QKV], bias_raw[:, 2, :]), 3)
                dve.wait_ge(gram_high.sem, 1)
                v.scalar_tensor_tensor(gram_l[:], ps_h[:], 1.0 / HID, gram_h[:].bitcast(F32),
                                       ALU.mult, ALU.subtract).then_inc(gram_done.sem, 1)
                dve.wait_ge(router_b_ps.sem, 1)
                link(v.tensor_copy(router_b[:], ps_o[:, 0:EXPERTS]))
                dve.wait_ge(vz_zeroed.sem, 2)

            def newton(k, s, value, guess, a, b, result):
                if k == 0:
                    v.scalar_tensor_tensor(a, guess, -0.5, guess, ALU.mult, ALU.mult).then_inc(s.sem, 1)
                elif k == 1:
                    v.tensor_tensor(b, value, a, ALU.mult).then_inc(s.sem, 1)
                else:
                    v.scalar_tensor_tensor(result, b, 1.5, guess, ALU.add, ALU.mult).then_inc(s.sem, 1)

            def newton1(m, k):
                if k == 0:
                    dve.wait_ge(s_root1_r.sem, s_root1_r.at(m, 1))
                else:
                    dve.wait_ge(s_root1.sem, s_root1.at(m, k))
                newton(k, s_root1, root1_in[:], root1_r[:], root1_a[:], root1_b[:], root1[:])

            def newton2(n, k):
                if k == 0:
                    dve.wait_ge(s_root2_r.sem, s_root2_r.at(n, 1))
                else:
                    dve.wait_ge(s_root2.sem, s_root2.at(n, k))
                newton(k, s_root2, root2_in[:], root2_r[:], root2_a[:], root2_b[:], root2[:])

            def input_stats(n, p):
                dve.wait_ge(x_loaded[p].sem, x_loaded[p].at(n - p, 16))
                for t in range(NT):
                    v.bn_stats(stats[:, NT + t, :], x_in[p][:, t, :]).then_inc(s_stats_x.sem, 1)

            def input_moments(n):
                for t in range(NT):
                    dve.wait_ge(s_stats_x.sem, s_stats_x.at(n, t + 1))
                    dve.nop(nofuse=True)
                    v.bn_aggr(mean_var[:, NT + t, :], stats[:, NT + t, :]).then_inc(s_mean_var_x.sem, 1)

            def root1_input(m, has_x, has_f):
                if has_x:
                    dve.wait_ge(s_mean_var_x.sem, s_mean_var_x.at(m, NT))
                if has_f:
                    dve.wait_ge(s_mean_var_f.sem, s_mean_var_f.at(m - 3, NT))
                v.tensor_scalar(root1_in[:, NM:], mean_var[:, :, 1], EPS_LN, None, ALU.add).then_inc(s_root1_in.sem, 1)

            def input_norm(n, p):
                dve.wait_ge(s_root1.sem, s_root1.at(n, 3))
                if s_base0.due(n - 2, 1):
                    dve.wait_ge(s_base0.sem, s_base0.at(n - 2, 1))
                for t in range(NT):
                    v.tensor_scalar(xn[p][:, t, :], x_in[p][:, t, :], mean_var[:, NT + t, 0:1], rstd_x[:, t:t + 1],
                                    ALU.subtract, ALU.mult).then_inc(s_xn.sem, 1)

            def router_var(n, p, k):
                if k == 0:
                    dve.wait_ge(s_root1.sem, s_root1.at(n, 3))
                    v.tensor_tensor(rt1[:], mean_var[:, NT:, 1], rstd_x, ALU.mult).then_inc(s_router_var.sem, 1)
                else:
                    dve.wait_ge(s_router_var.sem, s_router_var.at(n, 1))
                    v.tensor_tensor(var[p][:, NV:], rt1[:], rstd_x, ALU.mult).then_inc(s_router_var.sem, 1)

            def xt_low(n, p):
                dve.wait_ge(s_xt_h.sem, s_xt_h.at(n, 1))
                if s_hid.due(n - 2, NG):
                    dve.wait_ge(s_hid.sem, s_hid.at(n - 2, NG))
                v.tensor_tensor(xt_l[p][:], ps_a[:, 0:SEQ], xt_h[p][:].bitcast(F32),
                                ALU.subtract).then_inc(s_xt_l.sem, 1)

            def take_projections(n, p, t):
                dve.wait_ge(s_proj.sem, s_proj.at(n, t + 1))
                v.tensor_tensor(qk[:, t, :], ps_a[:, 0:2 * D], bias[:, 0:2 * D], ALU.add).then_inc(s_qk.sem, 1)
                if s_pv.due(n - 2, NG):
                    dve.wait_ge(s_pv.sem, s_pv.at(n - 2, NG))
                v_blocks = vz[p][:, t, :].rearrange("p (g s) -> p g s", g=NG)[:, :, 0:NC * 32]
                v_blocks = v_blocks.rearrange("p g (c s) -> p g c s", c=NC)[:, :, :, 0:DH]
                v.tensor_tensor(v_blocks, perm(ps_a[:, 2 * D:QKV]), perm(bias[:, 2 * D:QKV]),
                                ALU.add).then_inc(s_v.sem, 1)
                v.tensor_copy(logits0[:, t, :], ps_a[:, QKV:PROJ]).then_inc(s_logits0.sem, 1)

            def rope_cos(n):
                dve.wait_ge(s_qk.sem, s_qk.at(n, NT))
                v.tensor_tensor(rope1[:].rearrange("p (t h d) -> p t h d", t=NT, d=DH),
                                qk[:].rearrange("p t (h d) -> p t h d", d=DH),
                                cos_t[:].unsqueeze(2).to_broadcast([128, NT, 2 * HEADS, DH]),
                                ALU.mult).then_inc(s_rope1.sem, 1)

            def mean_squares(n, k):
                if k == 0:
                    dve.wait_ge(s_qk_sq.sem, s_qk_sq.at(n, 1))
                    v.tensor_reduce(ms_sum[:], qk_sq[:].rearrange("p t (h d) -> p (t h) d", d=DH), AX_X,
                                    ALU.add).then_inc(s_ms.sem, 1)
                else:
                    dve.wait_ge(s_ms.sem, s_ms.at(n, 1))
                    v.tensor_scalar(root1_in[:, 0:NM], ms_sum[:], 1.0 / DH, EPS_RMS, ALU.mult,
                                    ALU.add).then_inc(s_ms.sem, 1)

            def rope_sum(n):
                dve.wait_ge(s_rope1.sem, s_rope1.at(n, 1))
                dve.wait_ge(s_rope2.sem, s_rope2.at(n, 1))
                v.tensor_tensor(rope_qk[:], rope1[:], rope2[:], ALU.add).then_inc(s_rope_qk.sem, 1)

            def rms_norm(n):
                dve.wait_ge(s_root1.sem, s_root1.at(n + 1, 3))
                dve.wait_ge(s_rope_qk.sem, s_rope_qk.at(n, 1))
                v.tensor_tensor(qk_r[:].rearrange("p (h d) -> p h d", d=DH),
                                rope_qk[:].rearrange("p (h d) -> p h d", d=DH),
                                rms.unsqueeze(2).to_broadcast([128, NM, DH]), ALU.mult).then_inc(s_qk_r.sem, 1)

            def stack_low(n):
                dve.wait_ge(s_high.sem, s_high.at(n, 1))
                high_low = stack[:].rearrange("p t k h s d -> p (t k h) s d")
                v.tensor_tensor(high_low[:, :, 1, :], qk_r[:].rearrange("p (h d) -> p h d", d=DH),
                                high_low[:, :, 0, :], ALU.subtract).then_inc(s_low.sem, 1)

            def stack_k(n):
                dve.wait_ge(s_low.sem, s_low.at(n, 1))
                k_rows = stack[:, :, 1]
                v.tensor_copy(k_rows[:, :, :, 2:4, :].rearrange("p t h s d -> p t h (s d)"),
                              k_rows[:, :, :, 0:2, :].rearrange("p t h s d -> p t h (s d)")).then_inc(s_stack.sem, 1)

            def stack_q(n):
                q_rows = stack[:, :, 0]
                for t in range(NT):
                    last = v.tensor_copy(q_rows[:, t, :, 2:4, :], q_rows[:, t, :, 1::-1, :])
                last.then_inc(s_stack.sem, 1)

            def x_twice_low(n, p):
                dve.wait_ge(s_x_high.sem, s_x_high.at(n, 1))
                v.scalar_tensor_tensor(x_low2[p][:], xn[p][:], 2.0, x_hi[:].bitcast(F32), ALU.mult,
                                        ALU.subtract).then_inc(s_x_low2.sem, 1)

            def variances(n, p, t):
                dve.wait_ge(s_gram.sem, s_gram.at(n, t + 1))
                if t == 0:
                    dve.wait_ge(s_x_low2.sem, s_x_low2.at(n, 1))
                for e in range(EXPERTS):
                    k = t * EXPERTS + e
                    v.tensor_tensor_reduce(out=scrap[:, k, :], in0=ps_a[:, e * D:(e + 1) * D],
                                           in1=x_low2[p][:, t, :], scale=1.0, scalar=0.0, op0=ALU.mult,
                                           op1=ALU.add, accum_out=var[p][:, k:k + 1]).then_inc(s_var.sem, 1)

            def root2_input(n, p):
                dve.wait_ge(s_var.sem, s_var.at(n, NV))
                dve.wait_ge(s_router_var.sem, s_router_var.at(n, 2))
                v.tensor_scalar(root2_in[:], var[p][:], 0.0, EPS_LN, ALU.max, ALU.add).then_inc(s_root2_in.sem, 1)

            std3 = std[:].rearrange("p (t e) -> p t e", t=NT)
            std_high = std_cols[:, :, 0:EXPERTS]

            def hidden_std(n):
                dve.wait_ge(s_root2.sem, s_root2.at(n, 3))
                v.tensor_tensor(std[:], root2_in[:, 0:NV], root2[:, 0:NV], ALU.mult).then_inc(s_std.sem, 1)

            def std_columns(n, k):
                if k == 0:
                    dve.wait_ge(s_std.sem, s_std.at(n, 1))
                    if s_std_ps.due(n - 1, 1):
                        dve.wait_ge(s_std_ps.sem, s_std_ps.at(n - 1, 1))
                    v.tensor_copy(std_high.bitcast(F32R), std3).then_inc(s_std_cols.sem, 1)
                else:
                    dve.wait_ge(s_std_cols.sem, s_std_cols.at(n, 1))
                    v.tensor_tensor(std_cols[:, :, 32:32 + EXPERTS], std3, std_high,
                                    ALU.subtract).then_inc(s_std_cols.sem, 1)
                    v.tensor_copy(std_cols[:, :, 64:64 + EXPERTS], std_high).then_inc(s_std_cols.sem, 1)

            both, square = [128, NT, EXPERTS], [128, NT, EXPERTS, EXPERTS]

            def router_logits(n, k):
                if k == 0:
                    dve.wait_ge(s_root2.sem, s_root2.at(n, 3))
                    for t in range(NT):
                        v.scalar_tensor_tensor(lg2[:, t, :], logits0[:, t, :], root2[:, NV + t:NV + t + 1], router_b[:],
                                               ALU.mult, ALU.add).then_inc(s_lg.sem, 1)
                elif k == 1:
                    dve.wait_ge(s_lg.sem, s_lg.at(n, NT))
                    v.tensor_reduce(lg_max[:], lg2[:], AX_X, ALU.max).then_inc(s_lg.sem, 1)
                else:
                    dve.wait_ge(s_lg.sem, s_lg.at(n, NT + 1))
                    v.tensor_tensor(lg3[:], lg2[:], lg_max[:].unsqueeze(2).to_broadcast(both),
                                    ALU.subtract).then_inc(s_lg.sem, 1)

            def router_rank(n, k):
                if k == 0:
                    dve.wait_ge(s_lg.sem, s_lg.at(n, NT))
                    v.tensor_tensor(ahead[:], lg2[:].unsqueeze(2).to_broadcast(square),
                                    lg2[:].unsqueeze(3).to_broadcast(square), ALU.subtract).then_inc(s_rank.sem, 1)
                    return
                dve.wait_ge(s_rank.sem, s_rank.at(n, k))
                flat = "p t i j -> p (t i j)"
                if k == 1:
                    v.scalar_tensor_tensor(tied[:].rearrange(flat), ahead[:].rearrange(flat), 0.0,
                                           earlier.rearrange("p i j -> p (i j)").unsqueeze(1)
                                           .to_broadcast([128, NT, EXPERTS * EXPERTS]),
                                           ALU.is_equal, ALU.mult).then_inc(s_rank.sem, 1)
                elif k == 2:
                    v.scalar_tensor_tensor(beaten[:].rearrange(flat), ahead[:].rearrange(flat), 0.0,
                                           tied[:].rearrange(flat), ALU.is_gt, ALU.add).then_inc(s_rank.sem, 1)
                else:
                    v.tensor_reduce(rank[:], beaten[:].rearrange("p t i j -> p (t i) j"), AX_X,
                                    ALU.add).then_inc(s_rank.sem, 1)

            def gate_total(n):
                dve.wait_ge(s_gate.sem, s_gate.at(n, 1))
                v.tensor_reduce(gate_sum[:], gate[:], AX_X, ALU.add).then_inc(s_gate_sum.sem, 1)

            def router_weights(n, p, k):
                if k == 0:
                    dve.wait_ge(s_rank.sem, s_rank.at(n, 4))
                    v.scalar_tensor_tensor(chosen[:].rearrange("p t e -> p (t e)"), rank[:], 2.0,
                                           gate[:].rearrange("p t e -> p (t e)"), ALU.is_lt,
                                           ALU.mult).then_inc(s_weight.sem, 1)
                    return
                dve.wait_ge(s_weight.sem, s_weight.at(n, k))
                if k == 1:
                    v.tensor_reduce(chosen_sum[:], chosen[:], AX_X, ALU.add).then_inc(s_weight.sem, 1)
                elif k == 2:
                    dve.wait_ge(s_gate_sum.sem, s_gate_sum.at(n, 1))
                    v.scalar_tensor_tensor(gate_den[:], gate_sum[:], EPS_GATE, chosen_sum[:], ALU.mult,
                                           ALU.add).then_inc(s_weight.sem, 1)
                elif k == 3:
                    v.reciprocal(gate_inv[:], gate_den[:]).then_inc(s_weight.sem, 1)
                else:
                    for t in range(NT):
                        v.scalar_tensor_tensor(scale_e[p][:, t, :], chosen[:, t, :], gate_inv[:, t:t + 1],
                                               root2[:, t * EXPERTS:(t + 1) * EXPERTS], ALU.mult,
                                               ALU.mult).then_inc(s_scale_e.sem, 1)

            def combine(j, p, e, t):
                o = ps_o[:, t * D:(t + 1) * D]
                s = scale_e[p][:, t, e:e + 1]
                if e == 0:
                    if t == 0:
                        dve.wait_ge(s_expert.sem, s_expert.at(j, 1))
                        dve.wait_ge(s_scale_e.sem, s_scale_e.at(j, NT))
                        if s_ffn_n.due(j - 2, NT):
                            dve.wait_ge(s_ffn_n.sem, s_ffn_n.at(j - 2, NT))
                    v.tensor_scalar(acc[p][:, t, :], o, s, None, ALU.mult).then_inc(s_acc.sem, 1)
                    return
                if t == 0:
                    dve.wait_ge(s_expert.sem, s_expert.at(j, e + 1))
                if t == 0 and e == EXPERTS - 1:
                    dve.wait_ge(s_attn.sem, s_attn.at(j, 1))
                dve.wait_ge(s_acc.sem, s_acc.at(j, e * NT - NT + t + 1))
                v.scalar_tensor_tensor(acc[p][:, t, :], o, s, acc[p][:, t, :], ALU.mult, ALU.add).then_inc(s_acc.sem, 1)

            def add_attention(j, p):
                dve.wait_ge(s_base1.sem, s_base1.at(j, 1))
                if s_y.due(j - 1, 1):
                    dve.wait_ge(s_y.sem, s_y.at(j - 1, 1))
                v.tensor_tensor(base2[:].rearrange("p t d -> p (t d)"), ps_o[:, NT * D:2 * NT * D],
                                base1[p][:].rearrange("p t d -> p (t d)"), ALU.add).then_inc(s_base2.sem, 1)

            def output_stats(j, p):
                for t in range(NT):
                    dve.wait_ge(s_acc.sem, s_acc.at(j, (EXPERTS - 1) * NT + t + 1))
                    v.bn_stats(stats[:, t, :], acc[p][:, t, :]).then_inc(s_stats_f.sem, 1)

            def output_moments(j):
                for t in range(NT):
                    dve.wait_ge(s_stats_f.sem, s_stats_f.at(j, t + 1))
                    dve.nop(nofuse=True)
                    v.bn_aggr(mean_var[:, t, :], stats[:, t, :]).then_inc(s_mean_var_f.sem, 1)

            def output_norm(j, p):
                dve.wait_ge(s_root1.sem, s_root1.at(j + 3, 3))
                if s_ffn_g.due(j - 1, 1):
                    dve.wait_ge(s_ffn_g.sem, s_ffn_g.at(j - 1, 1))
                for t in range(NT):
                    v.tensor_scalar(ffn_n[:, t, :], acc[p][:, t, :], mean_var[:, t, 0:1], rstd_f[:, t:t + 1],
                                    ALU.subtract, ALU.mult).then_inc(s_ffn_n.sem, 1)

            def batch(j, p):
                h, n, m, q = j - 1, j + 1, j + 2, 1 - p
                has_h, has_j, has_n, has_m = exists(h), exists(j), exists(n), exists(m)
                if has_j:
                    std_columns(j, 1)
                    router_rank(j, 1)
                if has_h:
                    combine(h, q, 2, 0)
                    combine(h, q, 2, 1)
                if has_j:
                    router_rank(j, 2)
                    router_rank(j, 3)
                if has_n:
                    x_twice_low(n, q)
                    xt_low(n, q)
                if has_j:
                    router_logits(j, 2)
                if has_m:
                    input_stats(m, p)
                if has_j:
                    gate_total(j)
                if has_n:
                    router_var(n, q, 1)
                if has_h:
                    combine(h, q, 3, 0)
                    combine(h, q, 3, 1)
                if has_n:
                    take_projections(n, q, 0)
                if has_m:
                    input_moments(m)
                if has_h:
                    add_attention(h, q)
                    output_stats(h, q)
                if has_n:
                    take_projections(n, q, 1)
                if has_h:
                    output_moments(h)
                if has_n:
                    rope_cos(n)
                root1_input(m, exists(m), exists(m - 3))
                if has_j:
                    router_weights(j, p, 0)
                if has_n:
                    mean_squares(n, 0)
                    mean_squares(n, 1)
                    variances(n, q, 0)
                newton1(m, 0)
                if has_j:
                    router_weights(j, p, 1)
                newton1(m, 1)
                if has_n:
                    rope_sum(n)
                newton1(m, 2)
                if has_j:
                    router_weights(j, p, 2)
                if has_n:
                    rms_norm(n)
                    variances(n, q, 1)
                    stack_low(n)
                    root2_input(n, q)
                    stack_k(n)
                    stack_q(n)
                if has_j:
                    router_weights(j, p, 3)
                    router_weights(j, p, 4)
                    combine(j, p, 0, 0)
                    combine(j, p, 0, 1)
                if has_n:
                    newton2(n, 0)
                if has_m:
                    router_var(m, p, 0)
                if has_n:
                    newton2(n, 1)
                if has_h:
                    output_norm(h, q)
                if has_n:
                    newton2(n, 2)
                    hidden_std(n)
                    std_columns(n, 0)
                    router_logits(n, 0)
                if has_j:
                    combine(j, p, 1, 0)
                    combine(j, p, 1, 1)
                if has_n:
                    router_logits(n, 1)
                    router_rank(n, 0)
                if has_m:
                    input_norm(m, p)

            batches(dve, batch, {-2: setup_first, -1: setup_stage_a}, 1)

        @block.scalar
        def _(act):
            a = nc.scalar
            a.preload_act_table_set("natural_log_exp_and_others")

            def roots1(m, k):
                if k == 0:
                    act.wait_ge(s_root1_in.sem, s_root1_in.at(m, 1))
                    if exists(m - 1):
                        act.wait_ge(s_ms.sem, s_ms.at(m - 1, 2))
                    a.activation(root1_ln[:], root1_in[:], ACT.Ln).then_inc(s_root1_ln.sem, 1)
                else:
                    act.wait_ge(s_root1_ln.sem, s_root1_ln.at(m, 1))
                    a.activation(root1_r[:], root1_ln[:], ACT.Exp, scale=-0.5).then_inc(s_root1_r.sem, 1)

            def xt_high(n, p):
                act.wait_ge(s_xt.sem, s_xt.at(n, 1))
                if s_hid.due(n - 2, NG):
                    act.wait_ge(s_hid.sem, s_hid.at(n - 2, NG))
                a.activation(xt_h[p][:], ps_a[:, 0:SEQ], ACT.Copy).then_inc(s_xt_h.sem, 1)

            def squares(n):
                act.wait_ge(s_qk.sem, s_qk.at(n, NT))
                a.activation(qk_sq[:], qk[:], ACT.Square).then_inc(s_qk_sq.sem, 1)

            def roots2(n, k):
                if k == 0:
                    act.wait_ge(s_root2_in.sem, s_root2_in.at(n, 1))
                    a.activation(root2_ln[:], root2_in[:], ACT.Ln).then_inc(s_root2_ln.sem, 1)
                else:
                    act.wait_ge(s_root2_ln.sem, s_root2_ln.at(n, 1))
                    a.activation(root2_r[:], root2_ln[:], ACT.Exp, scale=-0.5).then_inc(s_root2_r.sem, 1)

            def x_high(n, p):
                act.wait_ge(s_xn.sem, s_xn.at(n, NT))
                if s_x_low2.due(n - 1, 1):
                    act.wait_ge(s_x_low2.sem, s_x_low2.at(n - 1, 1))
                a.activation(x_hi[:], xn[p][:], ACT.Copy).then_inc(s_x_high.sem, 1)

            def high_half(n):
                act.wait_ge(s_qk_r.sem, s_qk_r.at(n, 1))
                if s_stack_ps.due(n - 1, 2):
                    act.wait_ge(s_stack_ps.sem, s_stack_ps.at(n - 1, 2))
                a.activation(stack[:].rearrange("p t k h s d -> p (t k h) s d")[:, :, 0, :],
                             qk_r[:].rearrange("p (h d) -> p h d", d=DH), ACT.Copy).then_inc(s_high.sem, 1)

            def take_stacks(n, p, k):
                act.wait_ge(s_stack_ps.sem, s_stack_ps.at(n, k + 1))
                if k == 0 and s_scores.due(n - 2, 2 * NG):
                    act.wait_ge(s_scores.sem, s_scores.at(n - 2, 2 * NG))
                a.activation(qk_t[p][:, k * NG:(k + 1) * NG, :].rearrange("p g s -> p (g s)"),
                             ps_a[:].bitcast(F16), ACT.Copy).then_inc(s_qk_t.sem, 1)

            def take_std(n, p):
                act.wait_ge(s_std_ps.sem, s_std_ps.at(n, 1))
                if s_hid.due(n - 2, NG):
                    act.wait_ge(s_hid.sem, s_hid.at(n - 2, NG))
                a.activation(std_t[p][0:96, :], ps_a[0:96, 0:SEQ], ACT.Copy).then_inc(s_std_t.sem, 1)

            def gates(n):
                act.wait_ge(s_lg.sem, s_lg.at(n, 4))
                a.activation(gate[:], lg3[:], ACT.Exp).then_inc(s_gate.sem, 1)

            def square_scores(j, g, half):
                act.wait_ge(s_scores.sem, s_scores.at(j, 2 * g + half + 1))
                if half == 0 and s_pv.due(j, g - 1):
                    act.wait_ge(s_pv.sem, s_pv.at(j, g - 1))
                heads = slice(2 * half, 2 * half + 2)
                a.activation(probs[g % 2][:, heads, :], ps_s[:, heads, 0:3 * 128], ACT.Square,
                             scale=1.0 / (DH * QK_SCALE * QK_SCALE)).then_inc(s_probs.sem, 1)

            def relu(j, e):
                act.wait_ge(s_hid.sem, s_hid.at(j, e + 1))
                if s_expert.due(j, e - 1):
                    act.wait_ge(s_expert.sem, s_expert.at(j, e - 1))
                a.activation(hid_t[e % 2][:], ps_h[:], ACT.Relu).then_inc(s_relu.sem, 1)

            def take_z(j):
                act.wait_ge(s_pv.sem, s_pv.at(j, NG))
                if s_attn.due(j - 1, 1):
                    act.wait_ge(s_attn.sem, s_attn.at(j - 1, 1))
                a.activation(z_t[:], ps_z[:, 0:SEQ], ACT.Copy).then_inc(s_z_t.sem, 1)

            def batch(j, p):
                h, n, m, q = j - 1, j + 1, j + 2, 1 - p
                has_h, has_j, has_n, has_m = exists(h), exists(j), exists(n), exists(m)
                if has_j:
                    take_stacks(j, p, 1)
                if has_h:
                    take_z(h)
                if has_j:
                    take_std(j, p)
                if has_n:
                    x_high(n, q)
                    xt_high(n, q)
                if has_j:
                    square_scores(j, 0, 0)
                    gates(j)
                    square_scores(j, 0, 1)
                    relu(j, 0)
                    square_scores(j, 1, 0)
                if has_n:
                    squares(n)
                if has_j:
                    square_scores(j, 1, 1)
                roots1(m, 0)
                roots1(m, 1)
                if has_j:
                    relu(j, 1)
                    square_scores(j, 2, 0)
                    square_scores(j, 2, 1)
                if has_n:
                    high_half(n)
                if has_j:
                    relu(j, 2)
                    square_scores(j, 3, 0)
                if has_n:
                    roots2(n, 0)
                    roots2(n, 1)
                if has_j:
                    square_scores(j, 3, 1)
                if has_n:
                    take_stacks(n, q, 0)
                if has_j:
                    relu(j, 3)

            def setup_first():
                act.wait_ge(loaded_w1.sem, loaded_w1.per)
                a.activation(ident16[:], ident, ACT.Copy).then_inc(ident16_done.sem, 1)
                half = EXPERTS * CH // 2
                for b in range(2):
                    act.wait_ge(w1_ct_ps.sem, b + 1)
                    a.activation(w1_ct[:, b * half:(b + 1) * half].rearrange("p c d -> p (c d)"), ps_s[:, 2 + b, :],
                                 ACT.Copy).then_inc(w1_ct_taken.sem, 1)

            def setup_stage_a():
                act.wait_ge(w1_scaled.sem, 1)
                a.activation(w1_h[:], w1_g[:].rearrange("p e h -> p (e h)"), ACT.Copy).then_inc(w1_high.sem, 1)
                act.wait_ge(b_masked.sem, 1)
                a.activation(b_rows[:], b_own[:].rearrange("p e h -> p (e h)"), ACT.Copy).then_inc(b_high.sem, 1)
                act.wait_ge(gram_ps.sem, 1)
                a.activation(gram_h[:], ps_h[:], ACT.Copy, scale=1.0 / HID).then_inc(gram_high.sem, 1)

            batches(act, batch, {-2: setup_first, -1: setup_stage_a}, 1)

        @block.gpsimd
        def _(pool):
            g_ = nc.gpsimd

            def mask(j, g, half):
                pool.wait_ge(s_probs.sem, s_probs.at(j, 2 * g + half + 1))
                pool.nop(nofuse=True)
                diagonal = probs[g % 2][:, 2 * half:2 * half + 2, 0:2 * 128]
                g_.affine_select(out=diagonal, in_=diagonal, compare_op=ALU.is_ge, fill=0.0, base=0,
                                 pattern=[[0, 2], [0, 2], [1, 128]],
                                 channel_multiplier=-1).then_inc(s_masked.sem, 1)

            def rope_sin(n):
                pool.wait_ge(s_qk.sem, s_qk.at(n, NT))
                pairs = "p (t h a two) -> p t h a two"
                g_.tensor_tensor(rope2[:].rearrange(pairs, t=NT, a=DH // 2, two=2),
                                 qk[:].rearrange("p t (h a two) -> p t h a two", a=DH // 2, two=2)[:, :, :, :, ::-1],
                                 sin_t[:].rearrange("p t (a two) -> p t a two", two=2).unsqueeze(2)
                                 .to_broadcast([128, NT, 2 * HEADS, DH // 2, 2]),
                                 ALU.mult).then_inc(s_rope2.sem, 1)

            def residual(n, p, k):
                if k == 0:
                    pool.wait_ge(s_xn.sem, s_xn.at(n, NT))
                    if s_base1.due(n - 1, 1):
                        pool.wait_ge(s_base1.sem, s_base1.at(n - 1, 1))
                    g_.tensor_tensor(base0[:], x_in[p][:], xn[p][:], ALU.add).then_inc(s_base0.sem, 1)
                else:
                    pool.wait_ge(s_base0.sem, s_base0.at(n, 1))
                    if s_base2.due(n - 2, 1):
                        pool.wait_ge(s_base2.sem, s_base2.at(n - 2, 1))
                    g_.tensor_tensor(base1[p][:], base0[:], on_gb[:, 1:2, :].to_broadcast([128, NT, D]),
                                     ALU.add).then_inc(s_base1.sem, 1)

            def finish(j, p, k):
                if k == 0:
                    pool.wait_ge(s_ffn_n.sem, s_ffn_n.at(j, NT))
                    g_.tensor_tensor(ffn_g[:], ffn_n[:], on_gb[:, 0:1, :].to_broadcast([128, NT, D]),
                                     ALU.mult).then_inc(s_ffn_g.sem, 1)
                else:
                    pool.wait_ge(s_ffn_g.sem, s_ffn_g.at(j, 1))
                    pool.wait_ge(s_base2.sem, s_base2.at(j, 1))
                    if y_stored[p].due(j - 2 - p, 16):
                        pool.wait_ge(y_stored[p].sem, y_stored[p].at(j - 2 - p, 16))
                    g_.tensor_tensor(y[p][:], ffn_g[:], base2[:], ALU.add).then_inc(s_y.sem, 1)

            def batch(j, p):
                h, n, m, q = j - 1, j + 1, j + 2, 1 - p
                has_h, has_j, has_n, has_m = exists(h), exists(j), exists(n), exists(m)
                if has_j:
                    mask(j, 0, 0)
                    mask(j, 0, 1)
                    residual(j, p, 1)
                    mask(j, 1, 0)
                if has_n:
                    residual(n, q, 0)
                    rope_sin(n)
                if has_j:
                    mask(j, 1, 1)
                    mask(j, 2, 0)
                    mask(j, 2, 1)
                    mask(j, 3, 0)
                    mask(j, 3, 1)
                if has_h:
                    finish(h, q, 0)
                    finish(h, q, 1)

            def setup_first():
                g_.memset(b_raw[:], 0.0).then_inc(b_zeroed.sem, 1)
                for p in range(2):
                    g_.memset(vz[p][:], 0.0).then_inc(vz_zeroed.sem, 1)

            def setup_stage_b():
                pool.wait_ge(w1_centred.sem, 1)
                pool.wait_ge(loaded_ln.sem, loaded_ln.per)
                g_.tensor_tensor(w1_g[:], w1_c[:], ln_g_all[:], ALU.mult).then_inc(w1_scaled.sem, 1)
                pool.wait_ge(loaded_b.sem, loaded_b.per)
                g_.tensor_tensor(b_own[:], b_raw[:], own_block.unsqueeze(2).to_broadcast([128, EXPERTS, HID]),
                                 ALU.mult).then_inc(b_masked.sem, 1)
                pool.wait_ge(w1_high.sem, 1)
                pool.wait_ge(w1_scaled.sem, 1)
                g_.tensor_tensor(w1_l[:], w1_g[:].rearrange("p e h -> p (e h)"), w1_h[:].bitcast(F32),
                                 ALU.subtract).then_inc(w1_done.sem, 1)
                pool.wait_ge(b_high.sem, 1)
                pool.wait_ge(b_masked.sem, 1)
                pool.wait_ge(w1_done.sem, 1)
                g_.tensor_tensor(b_rows[64:96, :], b_own[64:96].rearrange("p e h -> p (e h)"),
                                 b_rows[64:96, :].bitcast(F32), ALU.subtract).then_inc(b_done.sem, 1)
                pool.wait_ge(b_done.sem, 1)
                pool.wait_ge(loaded_out.sem, loaded_out.per)

            batches(pool, batch, {-2: setup_first, -1: setup_stage_b}, 1)

        @block.tensor
        def _(pe):
            t_ = nc.tensor

            def setup_stage_a():
                pe.wait_ge(w1_centred.sem, 1)
                for c in range(EXPERTS * CH):
                    last = t_.transpose(ps_s[:, 2 + c // 4, (c % 4) * D:(c % 4 + 1) * D],
                                        w1_c[:].rearrange("p e h -> p (e h)")[:, c * 128:(c + 1) * 128], ident)
                    if c % 4 == 3:
                        last.then_inc(w1_ct_ps.sem, 1)
                pe.wait_ge(loaded_proj.sem, loaded_proj.per)
                for n in range(4):
                    t_.transpose(ps_s[:, 0, n * D:(n + 1) * D], w_raw[:, n, :], ident)
                t_.transpose(ps_s[:, 1, 0:EXPERTS], router_raw[:],
                             consts[0:EXPERTS, 0:EXPERTS]).then_inc(weights_ps.sem, 1)
                pe.wait_ge(w1_ct_taken.sem, 2)
                for e in range(EXPERTS):
                    for c in range(CH):
                        w_t = w1_ct[:, e * CH + c, :]
                        last = t_.matmul(ps_h[:, e * D:(e + 1) * D], w_t, w_t, start=(c == 0), stop=(c == CH - 1))
                last.then_inc(gram_ps.sem, 1)
                pe.wait_ge(router_taken.sem, 1)
                t_.matmul(ps_o[:, 0:EXPERTS], rn_cols[:, 1:2].to_broadcast([128, 128]), router_t[:], start=True,
                          stop=True).then_inc(router_b_ps.sem, 1)
                pe.wait_ge(proj_done.sem, 1)
                pe.wait_ge(ident16_done.sem, 1)

            def setup_stage_b():
                pe.wait_ge(w1_done.sem, 1)
                pe.wait_ge(b_done.sem, 1)
                pe.wait_ge(loaded_out.sem, loaded_out.per)

            def three_passes(dst, stationary, moving, start=True, stop=True):
                (sh, sl), (mh, ml) = stationary, moving
                t_.matmul(dst, sh, mh, start=start, stop=False)
                t_.matmul(dst, sh, ml, start=False, stop=False)
                return t_.matmul(dst, sl, mh, start=False, stop=stop)

            def x_halves(p, t):
                cols = slice(t * 128, (t + 1) * 128)
                return xt_h[p][:, cols], xt_l[p][:, cols]

            def transpose_x(n, p):
                pe.wait_ge(s_xn.sem, s_xn.at(n, NT))
                if s_std_t.due(n - 1, 1):
                    pe.wait_ge(s_std_t.sem, s_std_t.at(n - 1, 1))
                for t in range(NT):
                    last = t_.transpose(ps_a[:, t * 128:(t + 1) * 128], xn[p][:, t, :], ident)
                last.then_inc(s_xt.sem, 1)

            def project(n, p, t):
                if t == 0:
                    pe.wait_ge(s_xt_l.sem, s_xt_l.at(n, 1))
                else:
                    pe.wait_ge(s_logits0.sem, s_logits0.at(n, t))
                three_passes(ps_a[:, 0:PROJ], x_halves(p, t), (proj_h[:], proj_l[:])).then_inc(s_proj.sem, 1)

            def gram(n, p, t):
                if t == 0:
                    if known(n) and n == 0:
                        pe.wait_ge(gram_done.sem, 1)
                    pe.wait_ge(s_logits0.sem, s_logits0.at(n, NT))
                else:
                    pe.wait_ge(s_var.sem, s_var.at(n, t * EXPERTS))
                x_high_t = x_halves(p, t)[0]
                t_.matmul(ps_a[:], x_high_t, gram_h[:], start=True, stop=False)
                t_.matmul(ps_a[:], x_high_t, gram_l[:], start=False, stop=True).then_inc(s_gram.sem, 1)

            def transpose_stacks(n, k):
                if k == 0:
                    pe.wait_ge(s_stack.sem, s_stack.at(n, 2))
                    pe.wait_ge(s_var.sem, s_var.at(n, NV))
                else:
                    pe.wait_ge(s_qk_t.sem, s_qk_t.at(n, 1))
                dst = ps_a[:].bitcast(F16)
                for g in range(NG):
                    for t in range(NT):
                        at = g * SEQ + t * 128
                        rows = stack[:, t, k, g * NC:(g + 1) * NC].rearrange("p h s d -> p (h s d)")
                        last = t_.transpose(dst[:, at:at + 128], rows, ident16[:])
                last.then_inc(s_stack_ps.sem, 1)

            def transpose_std(n):
                pe.wait_ge(s_std_cols.sem, s_std_cols.at(n, 3))
                pe.wait_ge(s_qk_t.sem, s_qk_t.at(n, 2))
                for t in range(NT):
                    last = t_.transpose(ps_a[0:96, t * 128:(t + 1) * 128], std_cols[:, t, :], ident)
                last.then_inc(s_std_ps.sem, 1)

            def scores(j, p, g, half):
                if g == 0 and half == 0:
                    pe.wait_ge(s_qk_t.sem, s_qk_t.at(j, 2))
                if s_probs.due(j, 2 * g - 1 + half):
                    pe.wait_ge(s_probs.sem, s_probs.at(j, 2 * g - 1 + half))
                heads = range(2 * half, 2 * half + 2)
                for c in heads:
                    r = slice(32 * c, 32 * c + 32)
                    t_.matmul(ps_s[:, c, 128:384], qk_t[p][r, NG + g, 0:128], qk_t[p][r, g, :], start=True, stop=True)
                for c in heads:
                    r = slice(32 * c, 32 * c + 32)
                    last = t_.matmul(ps_s[:, c, 0:128], qk_t[p][r, NG + g, 128:256], qk_t[p][r, g, 128:256],
                                     start=True, stop=True)
                last.then_inc(s_scores.sem, 1)

            def weigh_values(j, p, g):
                pe.wait_ge(s_masked.sem, s_masked.at(j, 2 * g + 2))
                if g == 0:
                    if s_z_t.due(j - 1, 1):
                        pe.wait_ge(s_z_t.sem, s_z_t.at(j - 1, 1))
                for t in range(NT):
                    for c in range(NC):
                        at = (g * NC + c) * 32
                        q0 = 0 if t == 0 else 128
                        cols = slice(128, 384) if t == 0 else slice(0, 128)
                        last = t_.matmul(ps_z[32 * c:32 * c + 32, q0:SEQ], vz[p][:, t, at:at + 32],
                                         probs[g % 2][:, c, cols], start=(g == 0 and t == 0),
                                         stop=(g == NG - 1 and t == NT - 1), skip_group_check=True)
                last.then_inc(s_pv.sem, 1)

            def hidden(j, p, e):
                if e == 0:
                    pe.wait_ge(s_std_t.sem, s_std_t.at(j, 1))
                if s_relu.due(j, e):
                    pe.wait_ge(s_relu.sem, s_relu.at(j, e))
                for c in range(CH):
                    cols = slice((e * CH + c) * 128, (e * CH + c + 1) * 128)
                    dst = ps_h[:, c * SEQ:(c + 1) * SEQ]
                    three_passes(dst, (w1_h[:, cols], w1_l[:, cols]), (xt_h[p][:], xt_l[p][:]), stop=False)
                    last = t_.matmul(dst, b_rows[:, cols], std_t[p][:], start=False, stop=True)
                last.then_inc(s_hid.sem, 1)

            def expert_out(j, p, e):
                pe.wait_ge(s_relu.sem, s_relu.at(j, e + 1))
                if e == 0:
                    if s_base2.due(j - 1, 1):
                        pe.wait_ge(s_base2.sem, s_base2.at(j - 1, 1))
                else:
                    pe.wait_ge(s_acc.sem, s_acc.at(j, e * NT))
                for t in range(NT):
                    for c in range(CH):
                        at = c * SEQ + t * 128
                        last = t_.matmul(ps_o[:, t * D:(t + 1) * D], hid_t[e % 2][:, at:at + 128],
                                         w2_sb[:, e * CH + c, :], start=(c == 0), stop=(c == CH - 1))
                last.then_inc(s_expert.sem, 1)

            def attention_out(j):
                pe.wait_ge(s_z_t.sem, s_z_t.at(j, 1))
                pe.wait_ge(s_acc.sem, s_acc.at(j, (EXPERTS - 1) * NT))
                for t in range(NT):
                    at = (NT + t) * D
                    last = t_.matmul(ps_o[:, at:at + D], z_t[:, t * 128:(t + 1) * 128], wo_t[:],
                                     start=True, stop=True)
                last.then_inc(s_attn.sem, 1)

            def batch(j, p):
                h, n, m, q = j - 1, j + 1, j + 2, 1 - p
                has_h, has_j, has_n, has_m = exists(h), exists(j), exists(n), exists(m)
                if has_h:
                    expert_out(h, q, 2)
                if has_j:
                    transpose_std(j)
                    scores(j, p, 0, 0)
                    scores(j, p, 0, 1)
                if has_n:
                    transpose_x(n, q)
                if has_h:
                    expert_out(h, q, 3)
                    attention_out(h)
                if has_n:
                    project(n, q, 0)
                if has_j:
                    hidden(j, p, 0)
                    scores(j, p, 1, 0)
                if has_n:
                    project(n, q, 1)
                if has_j:
                    weigh_values(j, p, 0)
                    scores(j, p, 1, 1)
                    scores(j, p, 2, 0)
                if has_n:
                    gram(n, q, 0)
                if has_j:
                    hidden(j, p, 1)
                    scores(j, p, 2, 1)
                    expert_out(j, p, 0)
                if has_n:
                    gram(n, q, 1)
                if has_j:
                    hidden(j, p, 2)
                    scores(j, p, 3, 0)
                    weigh_values(j, p, 1)
                    weigh_values(j, p, 2)
                    scores(j, p, 3, 1)
                if has_n:
                    transpose_stacks(n, 0)
                if has_j:
                    hidden(j, p, 3)
                    expert_out(j, p, 1)
                if has_n:
                    transpose_stacks(n, 1)
                if has_j:
                    weigh_values(j, p, 3)

            batches(pe, batch, {-1: setup_stage_a, 0: setup_stage_b}, 1)


def kernel(**inputs):
    import concourse.bacc as bacc
    from concourse.bass_utils import run_bass_kernel_spmd

    names = ["x", "Wq", "bq", "Wk", "bk", "Wv", "bv", "Wo", "norm_w"]
    names = [f"L0_attn_{n}" for n in names]
    names += [f"L0_ffn_{n}" for n in ("router_w", "rn_g", "rn_b", "w1", "ln_g", "ln_b", "w2", "on_g", "on_b")]
    inv_freq = (1.0 / np.float32(10000.0) ** (np.arange(0, DH, 2, dtype=np.float32) / np.float32(DH))).astype(np.float32)
    freqs = np.outer(np.arange(SEQ, dtype=np.float32), inv_freq).astype(np.float32)
    emb = np.concatenate([freqs, freqs], -1)
    sign = np.where(np.arange(DH) % 2 == 0, -1.0, 1.0).astype(np.float32)
    rope_c = np.stack([np.cos(emb), sign * np.sin(emb)]).astype(np.float32)
    rope_c = np.ascontiguousarray(rope_c.reshape(2, NT, 128, DH).transpose(2, 0, 1, 3))
    block = np.zeros((128, EXPERTS), np.float32)
    for quadrant in range(3):
        block[32 * quadrant:32 * quadrant + EXPERTS] = np.eye(EXPERTS, dtype=np.float32)
    earlier = np.broadcast_to(np.tril(np.ones((EXPERTS, EXPERTS), np.float32), -1).ravel(), (128, EXPERTS * EXPERTS))
    consts = {"constants": np.concatenate([np.eye(128, dtype=np.float32), rope_c.reshape(128, -1), earlier, block], 1)}
    nc = bacc.Bacc("TRN2", target_bir_lowering=False, num_devices=1)
    arrays, args = {}, []
    for name, a in [(n, np.ascontiguousarray(inputs[n])) for n in names] + list(consts.items()):
        arrays[f"in_{name}"] = a
        args.append(nc.dram_tensor(f"in_{name}", a.shape, mybir.dt.from_np(a.dtype), kind="ExternalInput").ap())
    out = nc.dram_tensor("out", (B, SEQ, D), F32, kind="ExternalOutput").ap()
    build(nc, *args, out)
    result = run_bass_kernel_spmd(nc, [arrays], core_ids=[0])
    return result.results[0]["out"]
```
